# Optimizing a Trainium2 kernel written in Bass

```python
import numpy as np
import jax
import jax.numpy as jnp

def _softmax(x, axis=-1):
    return jax.nn.softmax(x, axis=axis)

def _gelu(x):
    return jax.nn.gelu(x, approximate=True)

def _silu(x):
    return jax.nn.silu(x)

def _sigmoid(x):
    return jax.nn.sigmoid(x)

def _layernorm(x, axis=-1, eps=1e-05):
    m = jnp.mean(x, axis=axis, keepdims=True)
    v = jnp.var(x, axis=axis, keepdims=True)
    return (x - m) / jnp.sqrt(v + eps)

def _scatter_add(tgt, idx, src, axis=0):
    return tgt.at[idx].add(src)

def _segment_sum(src, seg, n):
    return jax.ops.segment_sum(src, seg, n)
kernel_name = 'mk_dlrm_tower_d1_rec_r8_c51ebe'

def setup_inputs(seed: int=0):
    np.random.seed(seed)
    _w = jnp.asarray

    def _rec_inputs():
        import jax
        import jax.numpy as jnp
        _tk = jax.random.key(seed)
        ids = jnp.stack([jax.random.randint(jax.random.fold_in(_tk, 200 + f), (2048,), 0, v, jnp.int32) for f, v in enumerate([1250, 1000, 1250, 12500, 12500, 12500, 12500, 1250, 12500, 12500, 1000, 125000, 1250, 1000, 1000, 1000, 1250, 12500, 1250, 1250, 1250, 12500, 1000, 1250, 1250, 1250])], axis=1)
        tbl_0 = 0.05 * jax.random.normal(jax.random.fold_in(_tk, 500 + 0), (1250, 128), jnp.float32)
        tbl_1 = 0.05 * jax.random.normal(jax.random.fold_in(_tk, 500 + 1), (1000, 128), jnp.float32)
        tbl_2 = 0.05 * jax.random.normal(jax.random.fold_in(_tk, 500 + 2), (1250, 128), jnp.float32)
        tbl_3 = 0.05 * jax.random.normal(jax.random.fold_in(_tk, 500 + 3), (12500, 128), jnp.float32)
        tbl_4 = 0.05 * jax.random.normal(jax.random.fold_in(_tk, 500 + 4), (12500, 128), jnp.float32)
        tbl_5 = 0.05 * jax.random.normal(jax.random.fold_in(_tk, 500 + 5), (12500, 128), jnp.float32)
        tbl_6 = 0.05 * jax.random.normal(jax.random.fold_in(_tk, 500 + 6), (12500, 128), jnp.float32)
        tbl_7 = 0.05 * jax.random.normal(jax.random.fold_in(_tk, 500 + 7), (1250, 128), jnp.float32)
        tbl_8 = 0.05 * jax.random.normal(jax.random.fold_in(_tk, 500 + 8), (12500, 128), jnp.float32)
        tbl_9 = 0.05 * jax.random.normal(jax.random.fold_in(_tk, 500 + 9), (12500, 128), jnp.float32)
        tbl_10 = 0.05 * jax.random.normal(jax.random.fold_in(_tk, 500 + 10), (1000, 128), jnp.float32)
        tbl_11 = 0.05 * jax.random.normal(jax.random.fold_in(_tk, 500 + 11), (125000, 128), jnp.float32)
        tbl_12 = 0.05 * jax.random.normal(jax.random.fold_in(_tk, 500 + 12), (1250, 128), jnp.float32)
        tbl_13 = 0.05 * jax.random.normal(jax.random.fold_in(_tk, 500 + 13), (1000, 128), jnp.float32)
        tbl_14 = 0.05 * jax.random.normal(jax.random.fold_in(_tk, 500 + 14), (1000, 128), jnp.float32)
        tbl_15 = 0.05 * jax.random.normal(jax.random.fold_in(_tk, 500 + 15), (1000, 128), jnp.float32)
        tbl_16 = 0.05 * jax.random.normal(jax.random.fold_in(_tk, 500 + 16), (1250, 128), jnp.float32)
        tbl_17 = 0.05 * jax.random.normal(jax.random.fold_in(_tk, 500 + 17), (12500, 128), jnp.float32)
        tbl_18 = 0.05 * jax.random.normal(jax.random.fold_in(_tk, 500 + 18), (1250, 128), jnp.float32)
        tbl_19 = 0.05 * jax.random.normal(jax.random.fold_in(_tk, 500 + 19), (1250, 128), jnp.float32)
        tbl_20 = 0.05 * jax.random.normal(jax.random.fold_in(_tk, 500 + 20), (1250, 128), jnp.float32)
        tbl_21 = 0.05 * jax.random.normal(jax.random.fold_in(_tk, 500 + 21), (12500, 128), jnp.float32)
        tbl_22 = 0.05 * jax.random.normal(jax.random.fold_in(_tk, 500 + 22), (1000, 128), jnp.float32)
        tbl_23 = 0.05 * jax.random.normal(jax.random.fold_in(_tk, 500 + 23), (1250, 128), jnp.float32)
        tbl_24 = 0.05 * jax.random.normal(jax.random.fold_in(_tk, 500 + 24), (1250, 128), jnp.float32)
        tbl_25 = 0.05 * jax.random.normal(jax.random.fold_in(_tk, 500 + 25), (1250, 128), jnp.float32)
        _rk = jax.random.fold_in(_tk, 7)
        r_dense_features = -0.000520686 + 1.00062 * jax.random.normal(jax.random.fold_in(_rk, 101), (2048, 128), jnp.float32)
        W_top1 = 0.0405887 * jax.random.normal(jax.random.fold_in(_tk, 801), (607, 512), jnp.float32)
        W_top2 = 0.0441942 * jax.random.normal(jax.random.fold_in(_tk, 802), (512, 256), jnp.float32)
        W_top3 = 0.0625 * jax.random.normal(jax.random.fold_in(_tk, 803), (256, 1), jnp.float32)
        b_top1 = jnp.zeros((512,), jnp.float32)
        b_top2 = jnp.zeros((256,), jnp.float32)
        return (r_dense_features, ids, tbl_0, tbl_1, tbl_2, tbl_3, tbl_4, tbl_5, tbl_6, tbl_7, tbl_8, tbl_9, tbl_10, tbl_11, tbl_12, tbl_13, tbl_14, tbl_15, tbl_16, tbl_17, tbl_18, tbl_19, tbl_20, tbl_21, tbl_22, tbl_23, tbl_24, tbl_25, W_top1, b_top1, W_top2, b_top2, W_top3)
    r_dense_features, ids, tbl_0, tbl_1, tbl_2, tbl_3, tbl_4, tbl_5, tbl_6, tbl_7, tbl_8, tbl_9, tbl_10, tbl_11, tbl_12, tbl_13, tbl_14, tbl_15, tbl_16, tbl_17, tbl_18, tbl_19, tbl_20, tbl_21, tbl_22, tbl_23, tbl_24, tbl_25, W_top1, b_top1, W_top2, b_top2, W_top3 = _rec_inputs()

    def _L0_rec_setup():
        import jax, jax.numpy as jnp
        import numpy as np
        F = 26
        N = F + 1
        _TRIU_I, _TRIU_J = np.triu_indices(N, k=1)
        key = jax.random.key(seed)
        k1, k2 = jax.random.split(key)
        B, D = (2048, 128)
        dense_features = jax.random.normal(k1, (B, D), dtype=jnp.float32)
        sparse_features = jax.random.normal(k2, (B, F, D), dtype=jnp.float32)
        return {'dense_features': dense_features, 'sparse_features': sparse_features}
    _L0_rec_all = _L0_rec_setup()
    _L0_rec_in = {k: v for k, v in _L0_rec_all.items() if k in ()}
    del _L0_rec_all
    return {'r_dense_features': r_dense_features, 'ids': ids, 'tbl_0': tbl_0, 'tbl_1': tbl_1, 'tbl_2': tbl_2, 'tbl_3': tbl_3, 'tbl_4': tbl_4, 'tbl_5': tbl_5, 'tbl_6': tbl_6, 'tbl_7': tbl_7, 'tbl_8': tbl_8, 'tbl_9': tbl_9, 'tbl_10': tbl_10, 'tbl_11': tbl_11, 'tbl_12': tbl_12, 'tbl_13': tbl_13, 'tbl_14': tbl_14, 'tbl_15': tbl_15, 'tbl_16': tbl_16, 'tbl_17': tbl_17, 'tbl_18': tbl_18, 'tbl_19': tbl_19, 'tbl_20': tbl_20, 'tbl_21': tbl_21, 'tbl_22': tbl_22, 'tbl_23': tbl_23, 'tbl_24': tbl_24, 'tbl_25': tbl_25, 'W_top1': W_top1, 'b_top1': b_top1, 'W_top2': W_top2, 'b_top2': b_top2, 'W_top3': W_top3}

def reference(r_dense_features, ids, tbl_0, tbl_1, tbl_2, tbl_3, tbl_4, tbl_5, tbl_6, tbl_7, tbl_8, tbl_9, tbl_10, tbl_11, tbl_12, tbl_13, tbl_14, tbl_15, tbl_16, tbl_17, tbl_18, tbl_19, tbl_20, tbl_21, tbl_22, tbl_23, tbl_24, tbl_25, W_top1, b_top1, W_top2, b_top2, W_top3):
    import jax
    import jax.numpy as jnp

    def _L0_rec_ref(dense_features, sparse_features):
        import jax, jax.numpy as jnp
        import numpy as np
        F = 26
        N = F + 1
        _TRIU_I, _TRIU_J = np.triu_indices(N, k=1)
        combined = jnp.concatenate([dense_features[:, None, :], sparse_features], axis=1)
        interactions = jnp.einsum('bnd,bmd->bnm', combined, combined)
        interactions_flat = interactions[:, _TRIU_I, _TRIU_J]
        return jnp.concatenate([dense_features, interactions_flat], axis=1)
    e = jnp.stack([tbl_0[ids[:, 0]], tbl_1[ids[:, 1]], tbl_2[ids[:, 2]], tbl_3[ids[:, 3]], tbl_4[ids[:, 4]], tbl_5[ids[:, 5]], tbl_6[ids[:, 6]], tbl_7[ids[:, 7]], tbl_8[ids[:, 8]], tbl_9[ids[:, 9]], tbl_10[ids[:, 10]], tbl_11[ids[:, 11]], tbl_12[ids[:, 12]], tbl_13[ids[:, 13]], tbl_14[ids[:, 14]], tbl_15[ids[:, 15]], tbl_16[ids[:, 16]], tbl_17[ids[:, 17]], tbl_18[ids[:, 18]], tbl_19[ids[:, 19]], tbl_20[ids[:, 20]], tbl_21[ids[:, 21]], tbl_22[ids[:, 22]], tbl_23[ids[:, 23]], tbl_24[ids[:, 24]], tbl_25[ids[:, 25]]], axis=1)
    z = _L0_rec_ref(r_dense_features, e)
    z = z.reshape(z.shape[0], -1)
    h = jnp.concatenate([z, r_dense_features], axis=1)
    h = jnp.maximum(h @ W_top1 + b_top1, 0.0)
    h = jnp.maximum(h @ W_top2 + b_top2, 0.0)
    y = h @ W_top3
    return y

_drawn_inputs = setup_inputs


def setup_inputs(seed=0):
    import zlib

    import numpy as np

    out = dict(_drawn_inputs(seed))
    spreads = {'b_top1': (0.0, 0.1), 'b_top2': (0.0, 0.1)}
    factors = {}
    for name, (base, spread) in spreads.items():
        noise = np.random.default_rng([zlib.crc32(name.encode()), seed]).standard_normal(out[name].shape)
        drawn = base * np.exp(spread * noise) if base else spread * noise
        out[name] = jnp.asarray(drawn.astype(out[name].dtype))
    for name, factor in factors.items():
        out[name] = (out[name] * factor).astype(out[name].dtype)
    return out
```

```python
from contextlib import ExitStack

import numpy as np

import concourse.bass as bass
from concourse import mybir

F32 = mybir.dt.float32
F32R = mybir.dt.float32r
I32 = mybir.dt.int32
ALU = mybir.AluOpType
ACT = mybir.ActivationFunctionType

P = 128
FEATURES = 26
VECTORS = FEATURES + 1
DIM = 128
BATCH = 2048
TILES = BATCH // P
TILES_PER_UNIT = 2
UNITS = TILES // TILES_PER_UNIT
UNIT = TILES_PER_UNIT * P

ONE_HOT = [1, 10, 13, 14, 15, 22, 0]
GATHERED = [f for f in range(FEATURES) if f not in ONE_HOT]
ONE_HOT_TABLES = len(ONE_HOT)
ORDER = [0] + [f + 1 for f in GATHERED] + [f + 1 for f in ONE_HOT]
TRANSPOSED = 1 + len(GATHERED)
PER_BANK = 4
BANKFULS = TRANSPOSED // PER_BANK

SLOT = 32
SAMPLES_PER_GROUP = P // SLOT
GROUPS = P // SAMPLES_PER_GROUP
UNIT_GROUPS = TILES_PER_UNIT * GROUPS
BATCH_GROUPS = 8
BATCHES = GROUPS // BATCH_GROUPS

ROW_STEP = VECTORS + 1
PAIR_J = VECTORS - 1
PAIR_K = (VECTORS - 1) // 2
PAIRS = VECTORS * (VECTORS - 1) // 2
PAIR_CHUNKS = 3
PAIR_ROWS = PAIRS // PAIR_CHUNKS
J_PER_CHUNK = PAIR_ROWS // PAIR_K

HIDDEN1 = 512
HIDDEN2 = 256
H1_CHUNKS = HIDDEN1 // P
H2_CHUNKS = HIDDEN2 // P

ONE_HOT_RING = 16
PREFILL = 8


def chunking(rows):
    chunks = -(-rows // P)
    while rows % chunks:
        chunks += 1
    return chunks, rows // chunks


def pair_rows():
    rows = []
    for c in range(PAIR_CHUNKS):
        js = range(c * J_PER_CHUNK, min((c + 1) * J_PER_CHUNK, PAIR_J))
        flat = [ROW_STEP * j + k for j in js for k in range(1, PAIR_K + 1)]
        rows += flat
    rows += [ROW_STEP * j + PAIR_K + 1 for j in range(PAIRS - PAIR_J * PAIR_K)]
    return [(x // VECTORS, x % VECTORS) for x in rows]


def top1_row_order():
    place = {}
    for n in range(VECTORS):
        for m in range(n + 1, VECTORS):
            place[n, m] = DIM + len(place)
    pairs = []
    for n, m in pair_rows():
        a, b = sorted((ORDER[n], ORDER[m]))
        pairs.append(place[a, b])
    return list(range(DIM)) + list(range(DIM + PAIRS, 2 * DIM + PAIRS)) + pairs


def dlrm_tower(nc, dense, ids, one_hot_ids, tables, w1, w2, mlp_columns, out):
    chunks_of, rows_of = zip(*(chunking(tables[f].shape[0]) for f in ONE_HOT))
    total_chunks = sum(chunks_of)
    first_chunk = [sum(chunks_of[:k]) for k in range(ONE_HOT_TABLES)]
    max_chunks = max(chunks_of)
    chunk_kinds = sorted(set(chunks_of))
    half_tables = (ONE_HOT_TABLES + 1) // 2

    dense_v = dense.rearrange("(p t) d -> p t d", t=TILES)
    ids_v = ids.rearrange("(p t) f -> p (t f)", t=TILES)
    out_v = out.rearrange("(p t) x -> p (t x)", t=TILES)
    w1_pairs = w1[2 * DIM :, :].rearrange("(c r) o -> r c o", r=PAIR_ROWS)
    products = nc.dram_tensor("products_scratch", [VECTORS * VECTORS, UNIT], F32).ap()
    products_store = products.rearrange("(n m) (s g) -> n m s g", m=VECTORS, g=UNIT_GROUPS)
    products_diag = products[0 : PAIR_J * ROW_STEP, :].rearrange("(j k) x -> j k x", k=ROW_STEP)

    ctx = ExitStack()
    with ctx:

        def sb(name, shape, dt=F32):
            return ctx.enter_context(nc.sbuf_tensor(name, shape, dt))

        def pb(name, shape, dt=F32):
            return ctx.enter_context(nc.psum_tensor(name, shape, dt))

        def sem(name):
            return ctx.enter_context(nc.semaphore(name))

        ids_all = sb("ids_all", [P, TILES * FEATURES], I32)
        idx = sb("idx", [P, 2, TILES_PER_UNIT * FEATURES], I32)
        rows = sb("rows", [P, TILES_PER_UNIT, TRANSPOSED, DIM])
        identity = sb("identity", [P, P])
        E = sb("E", [P, 2, TILES_PER_UNIT, P * SLOT])
        staging = E[:, 1, :, :].rearrange("p j x -> p (j x)").rearrange("p (c d) -> p c d", d=DIM)
        table_hi = sb("table_hi", [P, total_chunks, DIM], F32R)
        table_lo = sb("table_lo", [P, total_chunks, DIM], F32R)
        row_number_i = sb("row_number_i", [P, len(chunk_kinds), max_chunks], I32)
        row_number = sb("row_number", [P, len(chunk_kinds), max_chunks])
        ids_spread = sb("ids_spread", [P, 2, ONE_HOT_TABLES, UNIT], I32)
        one_hot = sb("one_hot", [P, ONE_HOT_RING, UNIT], F32R)
        prods = sb("prods", [P, VECTORS, UNIT_GROUPS])
        dense_t = sb("dense_t", [P, 2, SAMPLES_PER_GROUP, TILES_PER_UNIT, GROUPS])
        pairs_t = sb("pairs_t", [P, PAIR_CHUNKS, UNIT])
        w1_dense = sb("w1_dense", [P, HIDDEN1])
        w1_pair = sb("w1_pair", [P, PAIR_CHUNKS, HIDDEN1])
        w2_sb = sb("w2_sb", [P, H1_CHUNKS, HIDDEN2])
        columns = sb("columns", [P, H1_CHUNKS + 2 * H2_CHUNKS])
        b1_sb = columns[:, :H1_CHUNKS]
        b2_sb = columns[:, H1_CHUNKS : H1_CHUNKS + H2_CHUNKS]
        w3_sb = columns[:, H1_CHUNKS + H2_CHUNKS :]
        h1 = sb("h1", [P, H1_CHUNKS, UNIT])
        w1_dense_parts = h1[:].rearrange("p c x -> p (c x)").rearrange("p (h o) -> p h o", h=2)
        h2 = sb("h2", [P, H2_CHUNKS, TILES_PER_UNIT, P])
        y = sb("y", [P, TILES])

        turned = [pb(f"turned{b}", [P, PER_BANK, P]) for b in range(2)]
        dots = [pb(f"dots{b}", [P, BATCH_GROUPS, P]) for b in range(2)]
        acc = [pb(f"acc{b}", [P, 2 * UNIT]) for b in range(2)]

        ids_landed = sem("ids_landed")
        idx_ready = sem("idx_ready")
        rows_landed = [[sem(f"rows_landed{j}_{g}") for g in range(BANKFULS)] for j in range(TILES_PER_UNIT)]
        dense_landed = sem("dense_landed")
        turned_done = [[sem(f"turned_done{j}_{g}") for g in range(BANKFULS)] for j in range(TILES_PER_UNIT)]
        turned_read = [sem(f"turned_read{b}") for b in range(2)]
        pads_zeroed = sem("pads_zeroed")
        identity_blank = sem("identity_blank")
        identity_ready = sem("identity_ready")
        iota_done = sem("iota_done")
        table_landed = [sem(f"table_landed{k}") for k in range(ONE_HOT_TABLES)]
        hi_done = sem("hi_done")
        lo_done = sem("lo_done")
        row_number_done = sem("row_number_done")
        spread0_landed = sem("spread0_landed")
        spread_landed = sem("spread_landed")
        one_hot_ready = sem("one_hot_ready")
        one_hot_used = sem("one_hot_used")
        mlp_done = sem("mlp_done")
        acc_read = sem("acc_read")
        dots_done = [sem(f"dots_done{b}") for b in range(2)]
        dots_read = [sem(f"dots_read{b}") for b in range(2)]
        prods_stored = sem("prods_stored")
        pairs_landed = sem("pairs_landed")
        weights_landed = sem("weights_landed")
        w1_dense_ready = sem("w1_dense_ready")
        out_stored = sem("out_stored")
        WEIGHT_LOADS = 4

        ACC_MLP = H1_CHUNKS + H2_CHUNKS + 1
        halves = [range(half_tables), range(half_tables, ONE_HOT_TABLES)]
        assert (ONE_HOT_TABLES + ACC_MLP) % 2 == 0

        def uses_before(u):
            if isinstance(u, int) and u == 0:
                return ONE_HOT_TABLES
            return u * (ONE_HOT_TABLES + ACC_MLP)

        def lookup_use(u, k):
            mlp_between = k >= half_tables and not (isinstance(u, int) and u == 0)
            return uses_before(u) + (k + (ACC_MLP if mlp_between else 0))

        def mlp_use(u):
            if isinstance(u, int) and u == UNITS - 1:
                return uses_before(u) + ACC_MLP
            return uses_before(u + 1) + (0 if isinstance(u, int) and u == UNITS - 2 else half_tables)

        def lookup_bank(u, k):
            return acc[lookup_use(0, k) % 2 if isinstance(u, int) and u == 0 else lookup_use(2, k) % 2]

        def mlp_bank(u, i):
            return acc[(mlp_use(u if isinstance(u, int) else 2) + i) % 2]

        READS = BATCHES * TILES_PER_UNIT // 2

        def e_out(q, j, n0, n):
            v = E[:, q, j, :].rearrange("p (g s n) -> p n s g", n=SLOT, s=SAMPLES_PER_GROUP)
            return v[:, n0 : n0 + n, :, :]

        def ahead(engine, count):
            if not isinstance(count, int):
                engine.compute_val(count)
            return count

        def wait(engine, semaphore, count):
            if not (isinstance(count, int) and count == 0):
                engine.wait_ge(semaphore, count)

        def all_units(engine, unit):
            unit(0, 0)
            with engine.Fori(0, UNITS // 2 - 1) as pair:
                for q in (1, 0):
                    unit(pair * 2 + (2 - q), q)
            unit(UNITS - 1, 1)

        block = ctx.enter_context(nc.Block())

        @block.gpsimd
        def _(pool):
            nc.gpsimd.memset(identity[:], 0.0).then_inc(identity_blank, 1)
            for kind, chunks in enumerate(chunk_kinds):
                nc.gpsimd.iota(
                    row_number_i[:, kind, :chunks], pattern=[[1, chunks]], base=0, channel_multiplier=chunks
                ).then_inc(iota_done, 1)
            pool.wait_ge(identity_blank, 1)
            nc.gpsimd.affine_select(
                out=identity[:], in_=identity[:], compare_op=ALU.not_equal, fill=1.0, base=0,
                pattern=[[-1, P]], channel_multiplier=1,
            ).then_inc(identity_ready, 1)
            pool.wait_ge(ids_landed, 16)

            def unit(u, q):
                nc.gpsimd.tensor_copy(
                    idx[:, q, :], ids_all[:, bass.ds(u * (TILES_PER_UNIT * FEATURES), TILES_PER_UNIT * FEATURES)]
                ).then_inc(idx_ready, 1)
                idx_count = ahead(pool, u + 1)
                for j in range(TILES_PER_UNIT):
                    for i, f in enumerate(GATHERED):
                        n = i + 1
                        if n == 1 or n % PER_BANK == 0:
                            pool.wait_ge(ids_landed, 16)
                            if j == 0 and n == 1:
                                pool.wait_ge(idx_ready, idx_count)
                            wait(pool, turned_done[j][n // PER_BANK], u)
                        col = j * FEATURES + f
                        pool.indirect_dma_start(
                            out=rows[:, j, n, :], out_offset=None, in_=tables[f],
                            in_offset=bass.IndirectOffsetOnAxis(ap=idx[:, q, col : col + 1], axis=0),
                        ).then_inc(rows_landed[j][n // PER_BANK], 16)

            all_units(pool, unit)

        @block.sync
        def _(sp):
            sp.dma_start(ids_all[:], ids_v).then_inc(ids_landed, 16)

            def load_spread(u, q):
                if not (isinstance(u, int) and u < 2):
                    made_count = ahead(sp, (u - 1) * total_chunks)
                    last_count = ahead(sp, (u - 1) * 16)
                    sp.wait_ge(table_landed[0], 16)
                    sp.wait_ge(one_hot_ready, made_count)
                    sp.wait_ge(spread_landed, last_count)
                sp.dma_start(
                    ids_spread[:, q, :, :].rearrange("p k x -> p (k x)"),
                    one_hot_ids[bass.ds(u, 1), :].partition_broadcast(P),
                ).then_inc(spread0_landed if isinstance(u, int) and u == 0 else spread_landed, 16)

            def load_dense(u):
                if not (isinstance(u, int) and u == 0):
                    turned_count = ahead(sp, u)
                    sp.wait_ge(table_landed[0], 16)
                    for j in range(TILES_PER_UNIT):
                        sp.wait_ge(turned_done[j][0], turned_count)
                sp.dma_start(
                    rows[:, :, 0, :], dense_v[:, bass.ds(u * TILES_PER_UNIT, TILES_PER_UNIT), :]
                ).then_inc(dense_landed, 16)

            def load_table(k):
                sp.dma_start(
                    staging[: rows_of[k], first_chunk[k] : first_chunk[k] + chunks_of[k], :],
                    tables[ONE_HOT[k]].rearrange("(r c) d -> r c d", c=chunks_of[k]),
                ).then_inc(table_landed[k], 16)

            load_table(0)
            load_spread(0, 0)
            load_table(1)
            load_dense(0)
            for k in range(2, ONE_HOT_TABLES):
                load_table(k)
            load_spread(1, 1)
            sp.dma_start(
                w1_dense_parts[:], w1[0 : 2 * DIM, :].rearrange("(h p) o -> p h o", p=DIM)
            ).then_inc(weights_landed, 16)
            sp.dma_start(w1_pair[:PAIR_ROWS], w1_pairs).then_inc(weights_landed, 16)
            sp.dma_start(w2_sb[:], w2.rearrange("(c p) o -> p c o", p=P)).then_inc(weights_landed, 16)
            sp.dma_start(columns[:], mlp_columns).then_inc(weights_landed, 16)

            def unit(u, q):
                if not (isinstance(u, int) and u == UNITS - 1):
                    load_dense(u + 1)
                    load_spread(u + 2, q)
                dots_count = ahead(sp, (u + 1) * READS)
                pairs_count = ahead(sp, u * 64)
                for b in range(2):
                    sp.wait_ge(dots_read[b], dots_count)
                wait(sp, pairs_landed, pairs_count)
                for s in range(SAMPLES_PER_GROUP):
                    sp.dma_start(
                        products_store[:, :, s, :], prods[s * SLOT : s * SLOT + VECTORS, :, :]
                    ).then_inc(prods_stored, 16)
                free_count = mlp_use(u - 1) + H1_CHUNKS if not (isinstance(u, int) and u == 0) else 0
                free_count = ahead(sp, free_count)
                sp.wait_ge(prods_stored, (u + 1) * 64)
                wait(sp, acc_read, free_count)
                for c in range(PAIR_CHUNKS):
                    j0 = c * J_PER_CHUNK
                    j1 = min(j0 + J_PER_CHUNK, PAIR_J)
                    sp.dma_start(
                        pairs_t[0 : (j1 - j0) * PAIR_K, c, :], products_diag[j0:j1, 1 : PAIR_K + 1, :]
                    ).then_inc(pairs_landed, 16)
                main = (PAIR_J - (PAIR_CHUNKS - 1) * J_PER_CHUNK) * PAIR_K
                sp.dma_start(
                    pairs_t[main:PAIR_ROWS, PAIR_CHUNKS - 1, :],
                    products_diag[0 : PAIR_ROWS - main, PAIR_K + 1, :],
                ).then_inc(pairs_landed, 16)

            all_units(sp, unit)
            sp.wait_ge(acc_read, mlp_use(UNITS - 1) + ACC_MLP)
            sp.dma_start(out_v, y[:]).then_inc(out_stored, 16)
            sp.wait_ge(out_stored, 16)

        def tile_steps(u, j):
            tables_left = [] if isinstance(u, int) and u == UNITS - 1 else list(halves[j])
            for g in range(BANKFULS):
                yield "turn", g
                if g % 2 == 1 and tables_left:
                    yield "look up", tables_left.pop(0)
            for k in tables_left:
                yield "look up", k

        def batch_quadrants(j, batch, b):
            g0 = j * GROUPS + batch * BATCH_GROUPS
            for s in range(SAMPLES_PER_GROUP):
                lo = s * SLOT
                src = dots[b][lo : lo + VECTORS, :, s * VECTORS : (s + 1) * VECTORS]
                dst = prods[lo : lo + VECTORS, :, g0 : g0 + BATCH_GROUPS].rearrange("p m g -> p g m")
                yield dst, src

        @block.scalar
        def _(act):
            def lookup_out(u, bank, q, k):
                act.wait_ge(one_hot_used, u * total_chunks + first_chunk[k] + chunks_of[k])
                n = TRANSPOSED + k
                for j in range(TILES_PER_UNIT):
                    dst = E[:, q, j, :].rearrange("p (g s n) -> p n s g", n=SLOT, s=SAMPLES_PER_GROUP)
                    last = nc.scalar.copy(
                        dst[:, n, :, :], bank[:, j * P : (j + 1) * P].rearrange("p (s g) -> p s g", g=GROUPS)
                    )
                last.then_inc(acc_read, 1)

            for k in range(ONE_HOT_TABLES):
                act.wait_ge(table_landed[k], 16)
                r, c, c0 = rows_of[k], chunks_of[k], first_chunk[k]
                nc.scalar.copy(
                    table_hi[:r, c0 : c0 + c, :], staging[:r, c0 : c0 + c, :]
                ).then_inc(hi_done, 1)
                if k >= 1:
                    lookup_out(0, acc[(k - 1) % 2], 0, k - 1)
            lookup_out(0, acc[(ONE_HOT_TABLES - 1) % 2], 0, ONE_HOT_TABLES - 1)

            def turn_out(u, q, j, g):
                act.wait_ge(turned_done[j][g], u + 1)
                bank = (j * BANKFULS + g) % 2
                src = turned[bank][:, :, :].rearrange("p n (s g) -> p n s g", g=GROUPS)
                if g == 0:
                    nc.scalar.copy(dense_t[:, q, :, j, :], src[:, 0, :, :])
                nc.scalar.copy(e_out(q, j, g * PER_BANK, PER_BANK), src).then_inc(turned_read[bank], 1)

            def mlp(u):
                act.wait_ge(weights_landed, 16 * WEIGHT_LOADS)
                for i in range(ACC_MLP):
                    act.wait_ge(mlp_done, u * ACC_MLP + (i + 1))
                    src = mlp_bank(u, i)
                    if i < H1_CHUNKS:
                        last = nc.scalar.activation(
                            h1[:, i, :], src[:, :UNIT], ACT.Relu, bias=b1_sb[:, i : i + 1]
                        )
                    elif i < H1_CHUNKS + H2_CHUNKS:
                        c = i - H1_CHUNKS
                        last = nc.scalar.activation(
                            h2[:, c, :, :].rearrange("p j (s g) -> p s j g", g=GROUPS),
                            src[:, :UNIT].rearrange("p (s j g) -> p s j g", j=TILES_PER_UNIT, g=GROUPS),
                            ACT.Relu, bias=b2_sb[:, c : c + 1],
                        )
                    else:
                        last = nc.scalar.copy(
                            y[:, bass.ds(u * TILES_PER_UNIT, TILES_PER_UNIT)], src[:, :TILES_PER_UNIT]
                        )
                    last.then_inc(acc_read, 1)

            def unit(u, q):
                for j in range(TILES_PER_UNIT):
                    for kind, x in tile_steps(u, j):
                        if kind == "turn":
                            turn_out(u, q, j, x)
                        else:
                            lookup_out(u + 1, lookup_bank(u, x), 1 - q, x)
                    if j == 0:
                        wait(act, prods_stored, u * 64)
                    for batch in range(0, BATCHES, 2):
                        act.wait_ge(dots_done[0], u * READS + ((j * BATCHES + batch) // 2 + 1))
                        for dst, src in batch_quadrants(j, batch, 0):
                            last = nc.scalar.copy(dst, src)
                        last.then_inc(dots_read[0], 1)
                    if j == 0 and not (isinstance(u, int) and u == 0):
                        mlp(u - 1)

            all_units(act, unit)
            mlp(UNITS - 1)

        one_hot_order = [(k, c) for k in range(ONE_HOT_TABLES) for c in range(chunks_of[k])]
        half_chunks = first_chunk[half_tables]
        assert half_chunks >= ONE_HOT_RING and total_chunks - half_chunks >= ONE_HOT_RING

        def ring_used(u, i):
            last = i - ONE_HOT_RING
            if last < 0:
                last = max(x for x in range(total_chunks) if x % ONE_HOT_RING == i) - total_chunks
            return u * total_chunks + last + 1

        @block.vector
        def _(dve):
            def one_hots(u, q, first, end):
                for i in range(first, end):
                    k, c = one_hot_order[i]
                    r = rows_of[k]
                    if not (isinstance(u, int) and u == 0 and i < ONE_HOT_RING):
                        dve.wait_ge(one_hot_used, ring_used(u, i))
                    kind = chunk_kinds.index(chunks_of[k])
                    nc.vector.tensor_scalar(
                        one_hot[:r, i % ONE_HOT_RING, :], ids_spread[:r, q, k, :], row_number[:r, kind, c : c + 1],
                        None, ALU.is_equal,
                    ).then_inc(one_hot_ready, 1)

            def zero_pads(q):
                nc.vector.memset(
                    E[:, q, :, :].rearrange("p j (x n) -> p (j x) n", n=SLOT)[:, :, VECTORS:SLOT], 0.0
                ).then_inc(pads_zeroed, 1)

            zero_pads(0)
            dve.wait_ge(iota_done, len(chunk_kinds))
            for kind, chunks in enumerate(chunk_kinds):
                nc.vector.tensor_copy(
                    row_number[:, kind, :chunks], row_number_i[:, kind, :chunks]
                ).then_inc(row_number_done, 1)
            dve.wait_ge(row_number_done, len(chunk_kinds))
            for k in range(ONE_HOT_TABLES):
                r, c, c0 = rows_of[k], chunks_of[k], first_chunk[k]
                dve.wait_ge(table_landed[k], 16)
                dve.wait_ge(hi_done, k + 1)
                nc.vector.tensor_tensor(
                    table_lo[:r, c0 : c0 + c, :], staging[:r, c0 : c0 + c, :],
                    table_hi[:r, c0 : c0 + c, :].bitcast(F32), ALU.subtract,
                ).then_inc(lo_done, 1)
                if k == 0:
                    dve.wait_ge(spread0_landed, 16)
                one_hots(0, 0, c0, c0 + c)
            dve.wait_ge(lo_done, ONE_HOT_TABLES)
            zero_pads(1)
            dve.wait_ge(spread_landed, 16)
            one_hots(1, 1, 0, PREFILL)
            dve.wait_ge(weights_landed, 16 * WEIGHT_LOADS)
            nc.vector.tensor_tensor(
                w1_dense[:], w1_dense_parts[:, 0, :], w1_dense_parts[:, 1, :], ALU.add
            ).then_inc(w1_dense_ready, 1)

            def unit(u, q):
                look_up = not (isinstance(u, int) and u == UNITS - 1)
                for j in range(TILES_PER_UNIT):
                    if look_up:
                        first, end = (PREFILL, half_chunks) if j == 0 else (half_chunks, total_chunks)
                        one_hots(u + 1, 1 - q, first, end)
                    if j == 0:
                        wait(dve, prods_stored, u * 64)
                    for batch in range(1, BATCHES, 2):
                        dve.wait_ge(dots_done[1], u * READS + ((j * BATCHES + batch) // 2 + 1))
                        for dst, src in batch_quadrants(j, batch, 1):
                            last = nc.vector.tensor_copy(dst, src)
                        last.then_inc(dots_read[1], 1)
                        if j == 1 and batch == 1 and look_up:
                            dve.wait_ge(spread_landed, (u + 2) * 16)
                            one_hots(u + 2, q, 0, PREFILL)

            all_units(dve, unit)

        @block.tensor
        def _(pe):
            def lookup(u, use, bank, k):
                c0 = first_chunk[k]
                if not (isinstance(use, int) and use < 2):
                    pe.wait_ge(acc_read, use - 1)
                for i in range(c0, c0 + chunks_of[k]):
                    r = rows_of[k]
                    pe.wait_ge(one_hot_ready, u * total_chunks + i + 1)
                    hot = one_hot[:r, i % ONE_HOT_RING, :]
                    nc.tensor.matmul(bank[:, :UNIT], table_hi[:r, i, :], hot, start=(i == c0), stop=False)
                    nc.tensor.matmul(
                        bank[:, :UNIT], table_lo[:r, i, :], hot, start=False, stop=(i == c0 + chunks_of[k] - 1)
                    ).then_inc(one_hot_used, 1)

            for k in range(ONE_HOT_TABLES):
                pe.wait_ge(lo_done, k + 1)
                lookup(0, k, acc[k % 2], k)
            pe.wait_ge(identity_ready, 1)
            pe.wait_ge(pads_zeroed, 2)

            def turn(u, j, g):
                i = j * BANKFULS + g
                if g == 0:
                    pe.wait_ge(dense_landed, (u + 1) * 16)
                    pe.wait_ge(rows_landed[j][g], (u + 1) * (16 * (PER_BANK - 1)))
                else:
                    pe.wait_ge(rows_landed[j][g], (u + 1) * (16 * PER_BANK))
                wait(pe, turned_read[i % 2], u * BANKFULS + i // 2)
                for n in range(PER_BANK):
                    last = nc.tensor.transpose(
                        turned[i % 2][:, n, :], rows[:, j, g * PER_BANK + n, :], identity[:]
                    )
                last.then_inc(turned_done[j][g], 1)

            def dot_products(u, q, j):
                if j == 0:
                    pe.wait_ge(acc_read, uses_before(u))
                for b in range(2):
                    i = (j + 1) * BANKFULS
                    pe.wait_ge(turned_read[b], u * BANKFULS + (i + 1 - b) // 2)
                for batch in range(BATCHES):
                    b = batch % 2
                    wait(pe, dots_read[b], u * READS + (j * BATCHES + batch) // 2)
                    for x in range(BATCH_GROUPS):
                        at = (batch * BATCH_GROUPS + x) * P
                        four = E[:, q, j, at : at + P]
                        last = nc.tensor.matmul(
                            dots[b][: P - SLOT + VECTORS, x, : SAMPLES_PER_GROUP * VECTORS].rearrange(
                                "p (s m) -> p s m", m=VECTORS
                            ),
                            four[:, : P - SLOT + VECTORS],
                            four.rearrange("p (s m) -> p s m", m=SLOT)[:, :, :VECTORS],
                            start=True, stop=True,
                        )
                    last.then_inc(dots_done[b], 1)

            def mlp(u, q):
                use = mlp_use(u)
                pe.wait_ge(w1_dense_ready, 1)
                pe.wait_ge(weights_landed, 16 * WEIGHT_LOADS)
                for i in range(H1_CHUNKS):
                    bank = mlp_bank(u, i)
                    pe.wait_ge(acc_read, use + (i - 1))
                    cols = slice(i * P, (i + 1) * P)
                    nc.tensor.matmul(
                        bank[:, :UNIT], w1_dense[:, cols], dense_t[:, q, :, :, :].rearrange("p s j g -> p (s j g)"),
                        start=True, stop=False,
                    )
                    if i == 0:
                        pe.wait_ge(pairs_landed, (u + 1) * 64)
                    for c in range(PAIR_CHUNKS):
                        last = nc.tensor.matmul(
                            bank[:, :UNIT], w1_pair[:PAIR_ROWS, c, cols], pairs_t[:PAIR_ROWS, c, :],
                            start=False, stop=(c == PAIR_CHUNKS - 1),
                        )
                    last.then_inc(mlp_done, 1)
                for i in range(H2_CHUNKS):
                    bank = mlp_bank(u, H1_CHUNKS + i)
                    for c in range(H1_CHUNKS):
                        pe.wait_ge(acc_read, use + (max(c + 1, H1_CHUNKS - 1) if i == 0 else H1_CHUNKS))
                        last = nc.tensor.matmul(
                            bank[:, :UNIT], w2_sb[:, c, i * P : (i + 1) * P], h1[:, c, :],
                            start=(c == 0), stop=(c == H1_CHUNKS - 1),
                        )
                    last.then_inc(mlp_done, 1)
                pe.wait_ge(acc_read, use + (H1_CHUNKS + H2_CHUNKS))
                bank = mlp_bank(u, H1_CHUNKS + H2_CHUNKS)
                for j in range(TILES_PER_UNIT):
                    for c in range(H2_CHUNKS):
                        last = nc.tensor.matmul(
                            bank[:, j : j + 1], h2[:, c, j, :], w3_sb[:, c : c + 1],
                            start=(c == 0), stop=(c == H2_CHUNKS - 1),
                        )
                last.then_inc(mlp_done, 1)

            def unit(u, q):
                for j in range(TILES_PER_UNIT):
                    for kind, x in tile_steps(u, j):
                        if kind == "turn":
                            turn(u, j, x)
                        else:
                            lookup(u + 1, lookup_use(u, x), lookup_bank(u, x), x)
                    dot_products(u, q, j)
                    if j == 0 and not (isinstance(u, int) and u == 0):
                        mlp(u - 1, 1 - q)

            all_units(pe, unit)
            mlp(UNITS - 1, 1)


def kernel(**inputs):
    import concourse.bacc as bacc
    from concourse.bass_utils import run_bass_kernel_spmd

    arrays = {k: np.ascontiguousarray(v) for k, v in inputs.items()}
    ids = arrays["ids"]
    spread = ids.reshape(P, UNITS, TILES_PER_UNIT, FEATURES)[:, :, :, ONE_HOT].transpose(1, 3, 2, 0)
    placed = {
        "dense_in": arrays["r_dense_features"],
        "ids_in": ids,
        "one_hot_ids_in": np.pad(spread.reshape(UNITS, ONE_HOT_TABLES * UNIT), ((0, 1), (0, 0))),
        "w1_in": np.ascontiguousarray(arrays["W_top1"][top1_row_order()]),
        "w2_in": arrays["W_top2"],
        "mlp_columns_in": np.concatenate(
            [arrays[name].reshape(-1, P).T for name in ("b_top1", "b_top2", "W_top3")], axis=1
        ),
    }
    placed.update({f"table{f}_in": arrays[f"tbl_{f}"] for f in range(FEATURES)})

    nc = bacc.Bacc("TRN2", target_bir_lowering=False, num_devices=1)
    ap = {
        name: nc.dram_tensor(name, a.shape, mybir.dt.from_np(a.dtype), kind="ExternalInput").ap()
        for name, a in placed.items()
    }
    out = nc.dram_tensor("out", (BATCH, 1), F32, kind="ExternalOutput").ap()
    dlrm_tower(
        nc, ap["dense_in"], ap["ids_in"], ap["one_hot_ids_in"], [ap[f"table{f}_in"] for f in range(FEATURES)],
        ap["w1_in"], ap["w2_in"], ap["mlp_columns_in"], out,
    )
    result = run_bass_kernel_spmd(nc, [placed], core_ids=[0])
    return result.results[0]["out"]
```

```python
from contextlib import ExitStack

import numpy as np

import concourse.bass as bass
from concourse import mybir

F32 = mybir.dt.float32
F32R = mybir.dt.float32r
I32 = mybir.dt.int32
ALU = mybir.AluOpType
ACT = mybir.ActivationFunctionType

P = 128
FEATURES = 26
VECTORS = FEATURES + 1
DIM = 128
BATCH = 2048
TILES = BATCH // P
TILES_PER_UNIT = 2
UNITS = TILES // TILES_PER_UNIT
UNIT = TILES_PER_UNIT * P

ONE_HOT = [1, 10, 13, 14, 15, 22, 0]
GATHERED = [f for f in range(FEATURES) if f not in ONE_HOT]
ONE_HOT_TABLES = len(ONE_HOT)
ORDER = [0] + [f + 1 for f in GATHERED] + [f + 1 for f in ONE_HOT]
TRANSPOSED = 1 + len(GATHERED)
PER_BANK = 4
BANKFULS = TRANSPOSED // PER_BANK

SLOT = 32
SAMPLES_PER_GROUP = P // SLOT
GROUPS = P // SAMPLES_PER_GROUP
UNIT_GROUPS = TILES_PER_UNIT * GROUPS
BATCH_GROUPS = 8
BATCHES = GROUPS // BATCH_GROUPS

ROW_STEP = VECTORS + 1
PAIR_J = VECTORS - 1
PAIR_K = (VECTORS - 1) // 2
PAIRS = VECTORS * (VECTORS - 1) // 2
PAIR_CHUNKS = 3
PAIR_ROWS = PAIRS // PAIR_CHUNKS
J_PER_CHUNK = PAIR_ROWS // PAIR_K

HIDDEN1 = 512
HIDDEN2 = 256
H1_CHUNKS = HIDDEN1 // P
H2_CHUNKS = HIDDEN2 // P

ONE_HOT_RING = 16
PREFILL = 8
BEFORE_SCORES = 10


def chunking(rows):
    chunks = -(-rows // P)
    while rows % chunks:
        chunks += 1
    return chunks, rows // chunks


def pair_rows():
    rows = []
    for c in range(PAIR_CHUNKS):
        js = range(c * J_PER_CHUNK, min((c + 1) * J_PER_CHUNK, PAIR_J))
        flat = [ROW_STEP * j + k for j in js for k in range(1, PAIR_K + 1)]
        rows += flat
    rows += [ROW_STEP * j + PAIR_K + 1 for j in range(PAIRS - PAIR_J * PAIR_K)]
    return [(x // VECTORS, x % VECTORS) for x in rows]


def top1_row_order():
    place = {}
    for n in range(VECTORS):
        for m in range(n + 1, VECTORS):
            place[n, m] = DIM + len(place)
    pairs = []
    for n, m in pair_rows():
        a, b = sorted((ORDER[n], ORDER[m]))
        pairs.append(place[a, b])
    return list(range(DIM)) + list(range(DIM + PAIRS, 2 * DIM + PAIRS)) + pairs


def dlrm_tower(nc, dense, ids, one_hot_ids, tables, w1, w2, mlp_columns, out):
    chunks_of, rows_of = zip(*(chunking(tables[f].shape[0]) for f in ONE_HOT))
    total_chunks = sum(chunks_of)
    first_chunk = [sum(chunks_of[:k]) for k in range(ONE_HOT_TABLES)]
    max_chunks = max(chunks_of)
    chunk_kinds = sorted(set(chunks_of))
    half_tables = (ONE_HOT_TABLES + 1) // 2

    dense_v = dense.rearrange("(p t) d -> p t d", t=TILES)
    ids_v = ids.rearrange("(p t) f -> p (t f)", t=TILES)
    out_v = out.rearrange("(p t) x -> p (t x)", t=TILES)
    w1_pairs = w1[2 * DIM :, :].rearrange("(c r) o -> r c o", r=PAIR_ROWS)
    products = nc.dram_tensor("products_scratch", [VECTORS * VECTORS, UNIT], F32).ap()
    products_store = products.rearrange("(n m) (s g) -> n m s g", m=VECTORS, g=UNIT_GROUPS)
    products_store_tile = products.rearrange("(n m) (j s g) -> n m j s g", m=VECTORS, j=TILES_PER_UNIT, g=GROUPS)
    products_diag = products[0 : PAIR_J * ROW_STEP, :].rearrange("(j k) x -> j k x", k=ROW_STEP)

    ctx = ExitStack()
    with ctx:

        def sb(name, shape, dt=F32):
            return ctx.enter_context(nc.sbuf_tensor(name, shape, dt))

        def pb(name, shape, dt=F32):
            return ctx.enter_context(nc.psum_tensor(name, shape, dt))

        def sem(name):
            return ctx.enter_context(nc.semaphore(name))

        ids_all = sb("ids_all", [P, TILES * FEATURES], I32)
        idx = sb("idx", [P, 2, TILES_PER_UNIT * FEATURES], I32)
        rows = sb("rows", [P, TILES_PER_UNIT, TRANSPOSED, DIM])
        identity = sb("identity", [P, P])
        E = sb("E", [P, 2, TILES_PER_UNIT, P * SLOT])
        staging = E[:, 1, :, :].rearrange("p j x -> p (j x)").rearrange("p (c d) -> p c d", d=DIM)
        table_hi = sb("table_hi", [P, total_chunks, DIM], F32R)
        table_lo = sb("table_lo", [P, total_chunks, DIM], F32R)
        row_number_i = sb("row_number_i", [P, len(chunk_kinds), max_chunks], I32)
        row_number = sb("row_number", [P, len(chunk_kinds), max_chunks])
        ids_spread = sb("ids_spread", [P, 2, ONE_HOT_TABLES, UNIT], I32)
        one_hot = sb("one_hot", [P, ONE_HOT_RING, UNIT], F32R)
        prods = sb("prods", [P, VECTORS, UNIT_GROUPS])
        dense_t = sb("dense_t", [P, 2, SAMPLES_PER_GROUP, TILES_PER_UNIT, GROUPS])
        pairs_t = sb("pairs_t", [P, PAIR_CHUNKS, UNIT])
        w1_dense = sb("w1_dense", [P, HIDDEN1])
        w1_pair = sb("w1_pair", [P, PAIR_CHUNKS, HIDDEN1])
        w2_sb = sb("w2_sb", [P, H1_CHUNKS, HIDDEN2])
        columns = sb("columns", [P, H1_CHUNKS + 2 * H2_CHUNKS])
        b1_sb = columns[:, :H1_CHUNKS]
        b2_sb = columns[:, H1_CHUNKS : H1_CHUNKS + H2_CHUNKS]
        w3_sb = columns[:, H1_CHUNKS + H2_CHUNKS :]
        h1 = sb("h1", [P, H1_CHUNKS, UNIT])
        w1_dense_parts = h1[:].rearrange("p c x -> p (c x)").rearrange("p (h o) -> p h o", h=2)
        h2 = sb("h2", [P, H2_CHUNKS, TILES_PER_UNIT, P])
        scores = sb("scores", [P, TILES_PER_UNIT, P])
        ones = sb("ones", [P, 1])
        y = sb("y", [P, TILES])

        turned = [pb(f"turned{b}", [P, PER_BANK, P]) for b in range(2)]
        dots = [pb(f"dots{b}", [P, BATCH_GROUPS, P]) for b in range(2)]
        acc = [pb(f"acc{b}", [P, 2 * UNIT]) for b in range(2)]

        ids_landed = sem("ids_landed")
        idx_ready = sem("idx_ready")
        rows_landed = [[sem(f"rows_landed{j}_{g}") for g in range(BANKFULS)] for j in range(TILES_PER_UNIT)]
        dense_landed = sem("dense_landed")
        turned_done = [[sem(f"turned_done{j}_{g}") for g in range(BANKFULS)] for j in range(TILES_PER_UNIT)]
        turned_read = [sem(f"turned_read{b}") for b in range(2)]
        pads_zeroed = sem("pads_zeroed")
        identity_blank = sem("identity_blank")
        identity_ready = sem("identity_ready")
        iota_done = sem("iota_done")
        table_landed = [sem(f"table_landed{k}") for k in range(ONE_HOT_TABLES)]
        hi_done = sem("hi_done")
        lo_done = sem("lo_done")
        row_number_done = sem("row_number_done")
        spread0_landed = sem("spread0_landed")
        spread_landed = sem("spread_landed")
        one_hot_ready = sem("one_hot_ready")
        one_hot_used = sem("one_hot_used")
        mlp_done = sem("mlp_done")
        ones_ready = sem("ones_ready")
        partial_scores_done = sem("partial_scores_done")
        scores_done = sem("scores_done")
        acc_read = sem("acc_read")
        dots_done = [sem(f"dots_done{b}") for b in range(2)]
        dots_read = [sem(f"dots_read{b}") for b in range(2)]
        prods_stored = sem("prods_stored")
        pairs_landed = sem("pairs_landed")
        weights_landed = sem("weights_landed")
        w1_dense_ready = sem("w1_dense_ready")
        out_stored = sem("out_stored")
        WEIGHT_LOADS = 4

        ACC_MLP = H1_CHUNKS + H2_CHUNKS + 1
        halves = [range(half_tables), range(half_tables, ONE_HOT_TABLES)]
        assert (ONE_HOT_TABLES + ACC_MLP) % 2 == 0

        def uses_before(u):
            if isinstance(u, int) and u == 0:
                return ONE_HOT_TABLES
            return u * (ONE_HOT_TABLES + ACC_MLP)

        def lookup_use(u, k):
            between = 0
            if not (isinstance(u, int) and u == 0):
                between = (ACC_MLP - 1) * (k >= half_tables) + (k > half_tables)
            return uses_before(u) + (k + between)

        def mlp_use(u):
            if isinstance(u, int) and u == UNITS - 1:
                return uses_before(u) + ACC_MLP
            return uses_before(u + 1) + (0 if isinstance(u, int) and u == UNITS - 2 else half_tables)

        def scores_bank(u):
            is_last = isinstance(u, int) and u == UNITS - 1
            return acc[(mlp_use(UNITS - 2 if is_last else 2) + ACC_MLP - is_last) % 2]

        def lookup_bank(u, k):
            return acc[lookup_use(0, k) % 2 if isinstance(u, int) and u == 0 else lookup_use(2, k) % 2]

        def mlp_bank(u, i):
            return acc[(mlp_use(u if isinstance(u, int) else 2) + i) % 2]

        READS = BATCHES * TILES_PER_UNIT // 2

        def e_out(q, j, n0, n):
            v = E[:, q, j, :].rearrange("p (g s n) -> p n s g", n=SLOT, s=SAMPLES_PER_GROUP)
            return v[:, n0 : n0 + n, :, :]

        def last_bank(j, i):
            return acc[(mlp_use(UNITS - 1) + j * ACC_MLP + i) % 2]

        def ahead(engine, count):
            if not isinstance(count, int):
                engine.compute_val(count)
            return count

        def wait(engine, semaphore, count):
            if not (isinstance(count, int) and count == 0):
                engine.wait_ge(semaphore, count)

        def all_units(engine, unit):
            unit(0, 0)
            with engine.Fori(0, UNITS // 2 - 1) as pair:
                for q in (1, 0):
                    unit(pair * 2 + (2 - q), q)
            unit(UNITS - 1, 1)

        block = ctx.enter_context(nc.Block())

        @block.gpsimd
        def _(pool):
            nc.gpsimd.memset(identity[:], 0.0).then_inc(identity_blank, 1)
            for kind, chunks in enumerate(chunk_kinds):
                nc.gpsimd.iota(
                    row_number_i[:, kind, :chunks], pattern=[[1, chunks]], base=0, channel_multiplier=chunks
                ).then_inc(iota_done, 1)
            pool.wait_ge(identity_blank, 1)
            nc.gpsimd.affine_select(
                out=identity[:], in_=identity[:], compare_op=ALU.not_equal, fill=1.0, base=0,
                pattern=[[-1, P]], channel_multiplier=1,
            ).then_inc(identity_ready, 1)
            pool.wait_ge(ids_landed, 16)

            def unit(u, q):
                nc.gpsimd.tensor_copy(
                    idx[:, q, :], ids_all[:, bass.ds(u * (TILES_PER_UNIT * FEATURES), TILES_PER_UNIT * FEATURES)]
                ).then_inc(idx_ready, 1)
                idx_count = ahead(pool, u + 1)
                for j in range(TILES_PER_UNIT):
                    for i, f in enumerate(GATHERED):
                        n = i + 1
                        if n == 1 or n % PER_BANK == 0:
                            pool.wait_ge(ids_landed, 16)
                            if j == 0 and n == 1:
                                pool.wait_ge(idx_ready, idx_count)
                            wait(pool, turned_done[j][n // PER_BANK], u)
                        col = j * FEATURES + f
                        pool.indirect_dma_start(
                            out=rows[:, j, n, :], out_offset=None, in_=tables[f],
                            in_offset=bass.IndirectOffsetOnAxis(ap=idx[:, q, col : col + 1], axis=0),
                        ).then_inc(rows_landed[j][n // PER_BANK], 16)

            all_units(pool, unit)

        def load_pairs(engine, part, cols):
            if part < PAIR_CHUNKS:
                j0 = part * J_PER_CHUNK
                j1 = min(j0 + J_PER_CHUNK, PAIR_J)
                dst = pairs_t[0 : (j1 - j0) * PAIR_K, part, cols]
                src = products_diag[j0:j1, 1 : PAIR_K + 1, cols]
            else:
                main = (PAIR_J - (PAIR_CHUNKS - 1) * J_PER_CHUNK) * PAIR_K
                dst = pairs_t[main:PAIR_ROWS, PAIR_CHUNKS - 1, cols]
                src = products_diag[0 : PAIR_ROWS - main, PAIR_K + 1, cols]
            engine.dma_start(dst, src).then_inc(pairs_landed, 16)

        def store_tile(engine, j, s):
            engine.dma_start(
                products_store_tile[:, :, j, s, :],
                prods[s * SLOT : s * SLOT + VECTORS, :, j * GROUPS : (j + 1) * GROUPS],
            ).then_inc(prods_stored, 16)

        @block.sync
        def _(sp):
            sp.dma_start(ids_all[:], ids_v).then_inc(ids_landed, 16)

            def load_spread(u, q):
                if not (isinstance(u, int) and u < 2):
                    made_count = ahead(sp, (u - 1) * total_chunks)
                    last_count = ahead(sp, (u - 1) * 16)
                    sp.wait_ge(table_landed[0], 16)
                    sp.wait_ge(one_hot_ready, made_count)
                    sp.wait_ge(spread_landed, last_count)
                sp.dma_start(
                    ids_spread[:, q, :, :].rearrange("p k x -> p (k x)"),
                    one_hot_ids[bass.ds(u, 1), :].partition_broadcast(P),
                ).then_inc(spread0_landed if isinstance(u, int) and u == 0 else spread_landed, 16)

            def load_dense(u):
                if not (isinstance(u, int) and u == 0):
                    turned_count = ahead(sp, u)
                    sp.wait_ge(table_landed[0], 16)
                    for j in range(TILES_PER_UNIT):
                        sp.wait_ge(turned_done[j][0], turned_count)
                sp.dma_start(
                    rows[:, :, 0, :], dense_v[:, bass.ds(u * TILES_PER_UNIT, TILES_PER_UNIT), :]
                ).then_inc(dense_landed, 16)

            def load_table(k):
                sp.dma_start(
                    staging[: rows_of[k], first_chunk[k] : first_chunk[k] + chunks_of[k], :],
                    tables[ONE_HOT[k]].rearrange("(r c) d -> r c d", c=chunks_of[k]),
                ).then_inc(table_landed[k], 16)

            load_table(0)
            load_spread(0, 0)
            load_table(1)
            load_dense(0)
            for k in range(2, ONE_HOT_TABLES):
                sp.wait_ge(table_landed[k - 2], 16)
                load_table(k)
            sp.wait_ge(table_landed[ONE_HOT_TABLES - 1], 16)
            load_spread(1, 1)
            sp.dma_start(
                w1_dense_parts[:], w1[0 : 2 * DIM, :].rearrange("(h p) o -> p h o", p=DIM)
            ).then_inc(weights_landed, 16)
            sp.dma_start(w1_pair[:PAIR_ROWS], w1_pairs).then_inc(weights_landed, 16)
            sp.dma_start(w2_sb[:], w2.rearrange("(c p) o -> p c o", p=P)).then_inc(weights_landed, 16)
            sp.dma_start(columns[:], mlp_columns).then_inc(weights_landed, 16)

            def unit(u, q):
                if not (isinstance(u, int) and u == UNITS - 1):
                    load_dense(u + 1)
                    load_spread(u + 2, q)
                if isinstance(u, int) and u == UNITS - 1:
                    return last_unit()
                dots_count = ahead(sp, (u + 1) * READS)
                pairs_count = ahead(sp, u * 64)
                for b in range(2):
                    sp.wait_ge(dots_read[b], dots_count)
                wait(sp, pairs_landed, pairs_count)
                for s in range(SAMPLES_PER_GROUP):
                    sp.dma_start(
                        products_store[:, :, s, :], prods[s * SLOT : s * SLOT + VECTORS, :, :]
                    ).then_inc(prods_stored, 16)
                free_count = mlp_use(u - 1) + H1_CHUNKS if not (isinstance(u, int) and u == 0) else 0
                free_count = ahead(sp, free_count)
                sp.wait_ge(prods_stored, (u + 1) * 64)
                wait(sp, acc_read, free_count)
                for part in range(PAIR_CHUNKS + 1):
                    load_pairs(sp, part, slice(0, UNIT))

            def last_unit():
                u = UNITS - 1
                for j in range(TILES_PER_UNIT):
                    for b in range(2):
                        sp.wait_ge(dots_read[b], u * READS + (j + 1) * READS // 2)
                    sp.wait_ge(pairs_landed, (u + j) * 64)
                    for s in range(SAMPLES_PER_GROUP):
                        store_tile(sp, j, s)
                    sp.wait_ge(prods_stored, (u + j + 1) * 64)
                    sp.wait_ge(acc_read, mlp_use(u - 1) + H1_CHUNKS)
                    for part in range(PAIR_CHUNKS + 1):
                        load_pairs(sp, part, slice(j * P, (j + 1) * P))

            all_units(sp, unit)
            sp.wait_ge(acc_read, mlp_use(UNITS - 1) + TILES_PER_UNIT * ACC_MLP)
            sp.dma_start(out_v, y[:]).then_inc(out_stored, 16)
            sp.wait_ge(out_stored, 16)

        def tile_steps(u, j):
            is_first, is_last = (isinstance(u, int) and u == x for x in (0, UNITS - 1))
            tables_left = [] if is_last else list(halves[j])
            for g in range(BANKFULS):
                if is_first and j == 0:
                    break
                yield "turn", g
                if g % 2 == 1 and tables_left:
                    yield "look up", tables_left.pop(0)
                if g == 1 and j == 1 and not is_first:
                    yield "scores", None
            for k in tables_left:
                yield "look up", k

        def batch_quadrants(j, batch, b):
            g0 = j * GROUPS + batch * BATCH_GROUPS
            for s in range(SAMPLES_PER_GROUP):
                lo = s * SLOT
                src = dots[b][lo : lo + VECTORS, :, s * VECTORS : (s + 1) * VECTORS]
                dst = prods[lo : lo + VECTORS, :, g0 : g0 + BATCH_GROUPS].rearrange("p m g -> p g m")
                yield dst, src

        @block.scalar
        def _(act):
            def lookup_out(u, bank, q, k):
                act.wait_ge(one_hot_used, u * total_chunks + first_chunk[k] + chunks_of[k])
                n = TRANSPOSED + k
                for j in range(TILES_PER_UNIT):
                    dst = E[:, q, j, :].rearrange("p (g s n) -> p n s g", n=SLOT, s=SAMPLES_PER_GROUP)
                    last = nc.scalar.copy(
                        dst[:, n, :, :], bank[:, j * P : (j + 1) * P].rearrange("p (s g) -> p s g", g=GROUPS)
                    )
                last.then_inc(acc_read, 1)

            def turn_out(u, q, j, g):
                act.wait_ge(turned_done[j][g], u + 1)
                bank = (j * BANKFULS + g) % 2
                src = turned[bank][:, :, :].rearrange("p n (s g) -> p n s g", g=GROUPS)
                if g == 0:
                    nc.scalar.copy(dense_t[:, q, :, j, :], src[:, 0, :, :])
                nc.scalar.copy(e_out(q, j, g * PER_BANK, PER_BANK), src).then_inc(turned_read[bank], 1)

            def prologue_out(k):
                lookup_out(0, acc[k % 2], 0, k)
                if 1 <= k <= BANKFULS:
                    turn_out(0, 0, 0, k - 1)

            for k in range(ONE_HOT_TABLES):
                act.wait_ge(table_landed[k], 16)
                r, c, c0 = rows_of[k], chunks_of[k], first_chunk[k]
                nc.scalar.copy(
                    table_hi[:r, c0 : c0 + c, :], staging[:r, c0 : c0 + c, :]
                ).then_inc(hi_done, 1)
                if k >= 1:
                    prologue_out(k - 1)
            prologue_out(ONE_HOT_TABLES - 1)

            def mlp(u, done, bank, cols):
                act.wait_ge(weights_landed, 16 * WEIGHT_LOADS)
                n = cols.stop - cols.start
                for i in range(ACC_MLP - 1):
                    act.wait_ge(mlp_done, done + (i + 1))
                    src = bank(i)[:, :n]
                    if i < H1_CHUNKS:
                        last = nc.scalar.activation(h1[:, i, cols], src, ACT.Relu, bias=b1_sb[:, i : i + 1])
                    else:
                        c = i - H1_CHUNKS
                        if i == H1_CHUNKS:
                            wait(act, scores_done, u)
                        if n == UNIT:
                            dst = h2[:, c, :, :].rearrange("p j (s g) -> p s j g", g=GROUPS)
                            src = src.rearrange("p (s j g) -> p s j g", j=TILES_PER_UNIT, g=GROUPS)
                        else:
                            dst = h2[:, c, cols.start // P, :]
                        last = nc.scalar.activation(dst, src, ACT.Relu, bias=b2_sb[:, c : c + 1])
                    last.then_inc(acc_read, 1)

            def score_out(done, bank, col, n):
                act.wait_ge(mlp_done, done + ACC_MLP)
                nc.scalar.copy(y[:, bass.ds(col, n)], bank[:, :n]).then_inc(acc_read, 1)

            def unit(u, q):
                for j in range(TILES_PER_UNIT):
                    for kind, x in tile_steps(u, j):
                        if kind == "turn":
                            turn_out(u, q, j, x)
                        elif kind == "scores":
                            score_out(
                                (u - 1) * ACC_MLP, scores_bank(u), (u - 1) * TILES_PER_UNIT, TILES_PER_UNIT
                            )
                        else:
                            lookup_out(u + 1, lookup_bank(u, x), 1 - q, x)
                    if j == 0:
                        wait(act, prods_stored, u * 64)
                    for batch in range(0, BATCHES, 2):
                        act.wait_ge(dots_done[0], u * READS + ((j * BATCHES + batch) // 2 + 1))
                        for dst, src in batch_quadrants(j, batch, 0):
                            last = nc.scalar.copy(dst, src)
                        last.then_inc(dots_read[0], 1)
                    if j == 0 and not (isinstance(u, int) and u == 0):
                        mlp(u - 1, (u - 1) * ACC_MLP, lambda i: mlp_bank(u - 1, i), slice(0, UNIT))

            def last_mlp(j):
                done = (UNITS - 1 + j) * ACC_MLP
                mlp(UNITS - 1 + j, done, lambda i: last_bank(j, i), slice(j * P, (j + 1) * P))
                score_out(done, last_bank(j, ACC_MLP - 1), (UNITS - 1) * TILES_PER_UNIT + j, 1)

            all_units(act, unit)
            last_mlp(0)
            last_mlp(1)

        one_hot_order = [(k, c) for k in range(ONE_HOT_TABLES) for c in range(chunks_of[k])]
        half_chunks = first_chunk[half_tables]
        assert half_chunks >= ONE_HOT_RING and total_chunks - half_chunks >= ONE_HOT_RING

        def ring_used(u, i):
            last = i - ONE_HOT_RING
            if last < 0:
                last = max(x for x in range(total_chunks) if x % ONE_HOT_RING == i) - total_chunks
            return u * total_chunks + last + 1

        @block.vector
        def _(dve):
            def one_hots(u, q, first, end):
                for i in range(first, end):
                    k, c = one_hot_order[i]
                    r = rows_of[k]
                    if not (isinstance(u, int) and u == 0 and i < ONE_HOT_RING):
                        dve.wait_ge(one_hot_used, ring_used(u, i))
                    kind = chunk_kinds.index(chunks_of[k])
                    nc.vector.tensor_scalar(
                        one_hot[:r, i % ONE_HOT_RING, :], ids_spread[:r, q, k, :], row_number[:r, kind, c : c + 1],
                        None, ALU.is_equal,
                    ).then_inc(one_hot_ready, 1)

            def zero_pads(q):
                nc.vector.memset(
                    E[:, q, :, :].rearrange("p j (x n) -> p (j x) n", n=SLOT)[:, :, VECTORS:SLOT], 0.0
                ).then_inc(pads_zeroed, 1)

            def make_scores(mlps, read, tile):
                dve.wait_ge(acc_read, read)
                wait(dve, mlp_done, mlps * ACC_MLP)
                nc.vector.tensor_scalar(
                    scores[:, tile, :], h2[:, 0, tile, :], w3_sb[:, 0:1], None, ALU.mult
                ).then_inc(partial_scores_done, 1)
                dve.wait_ge(partial_scores_done, mlps + 1)
                nc.vector.scalar_tensor_tensor(
                    scores[:, tile, :], h2[:, 1, tile, :], w3_sb[:, 1:2], scores[:, tile, :], ALU.mult, ALU.add
                ).then_inc(scores_done, 1)

            nc.vector.memset(ones[:], 1.0).then_inc(ones_ready, 1)
            zero_pads(0)
            dve.wait_ge(iota_done, len(chunk_kinds))
            for kind, chunks in enumerate(chunk_kinds):
                nc.vector.tensor_copy(
                    row_number[:, kind, :chunks], row_number_i[:, kind, :chunks]
                ).then_inc(row_number_done, 1)
            dve.wait_ge(row_number_done, len(chunk_kinds))
            for k in range(ONE_HOT_TABLES):
                r, c, c0 = rows_of[k], chunks_of[k], first_chunk[k]
                dve.wait_ge(table_landed[k], 16)
                dve.wait_ge(hi_done, k + 1)
                nc.vector.tensor_tensor(
                    table_lo[:r, c0 : c0 + c, :], staging[:r, c0 : c0 + c, :],
                    table_hi[:r, c0 : c0 + c, :].bitcast(F32), ALU.subtract,
                ).then_inc(lo_done, 1)
                if k == 0:
                    dve.wait_ge(spread0_landed, 16)
                one_hots(0, 0, c0, c0 + c)
            dve.wait_ge(lo_done, ONE_HOT_TABLES)
            zero_pads(1)
            dve.wait_ge(spread_landed, 16)
            one_hots(1, 1, 0, PREFILL)
            dve.wait_ge(weights_landed, 16 * WEIGHT_LOADS)
            nc.vector.tensor_tensor(
                w1_dense[:], w1_dense_parts[:, 0, :], w1_dense_parts[:, 1, :], ALU.add
            ).then_inc(w1_dense_ready, 1)

            def unit(u, q):
                look_up = not (isinstance(u, int) and u == UNITS - 1)
                for j in range(TILES_PER_UNIT):
                    first, end = (PREFILL, half_chunks) if j == 0 else (half_chunks, total_chunks)
                    if j == 1 and not (isinstance(u, int) and u == 0):
                        if look_up:
                            one_hots(u + 1, 1 - q, first, first + BEFORE_SCORES)
                            first += BEFORE_SCORES
                        make_scores(u - 1, mlp_use(u - 1) + (ACC_MLP - 1), slice(0, TILES_PER_UNIT))
                    if look_up:
                        one_hots(u + 1, 1 - q, first, end)
                    if j == 0:
                        wait(dve, prods_stored, u * 64)
                    for batch in range(1, BATCHES, 2):
                        dve.wait_ge(dots_done[1], u * READS + ((j * BATCHES + batch) // 2 + 1))
                        for dst, src in batch_quadrants(j, batch, 1):
                            last = nc.vector.tensor_copy(dst, src)
                        last.then_inc(dots_read[1], 1)
                        if j == 1 and batch == 1 and look_up:
                            dve.wait_ge(spread_landed, (u + 2) * 16)
                            one_hots(u + 2, q, 0, PREFILL)

            all_units(dve, unit)
            for j in range(TILES_PER_UNIT):
                make_scores(
                    UNITS - 1 + j, mlp_use(UNITS - 1) + (j + 1) * ACC_MLP - 1, slice(j, j + 1)
                )

        @block.tensor
        def _(pe):
            def lookup(u, use, bank, k):
                c0 = first_chunk[k]
                if not (isinstance(use, int) and use < 2):
                    pe.wait_ge(acc_read, use - 1)
                for i in range(c0, c0 + chunks_of[k]):
                    r = rows_of[k]
                    pe.wait_ge(one_hot_ready, u * total_chunks + i + 1)
                    hot = one_hot[:r, i % ONE_HOT_RING, :]
                    nc.tensor.matmul(bank[:, :UNIT], table_hi[:r, i, :], hot, start=(i == c0), stop=False)
                    nc.tensor.matmul(
                        bank[:, :UNIT], table_lo[:r, i, :], hot, start=False, stop=(i == c0 + chunks_of[k] - 1)
                    ).then_inc(one_hot_used, 1)

            def turn(u, j, g):
                i = j * BANKFULS + g
                if g == 0:
                    pe.wait_ge(dense_landed, (u + 1) * 16)
                    pe.wait_ge(rows_landed[j][g], (u + 1) * (16 * (PER_BANK - 1)))
                else:
                    pe.wait_ge(rows_landed[j][g], (u + 1) * (16 * PER_BANK))
                wait(pe, turned_read[i % 2], u * BANKFULS + i // 2)
                for n in range(PER_BANK):
                    last = nc.tensor.transpose(
                        turned[i % 2][:, n, :], rows[:, j, g * PER_BANK + n, :], identity[:]
                    )
                last.then_inc(turned_done[j][g], 1)

            pe.wait_ge(identity_ready, 1)
            for k in range(ONE_HOT_TABLES):
                pe.wait_ge(lo_done, k + 1)
                lookup(0, k, acc[k % 2], k)
                if 1 <= k <= BANKFULS:
                    turn(0, 0, k - 1)
            pe.wait_ge(pads_zeroed, 2)
            pe.wait_ge(ones_ready, 1)

            def dot_products(u, q, j):
                if j == 0:
                    pe.wait_ge(acc_read, uses_before(u))
                for b in range(2):
                    i = (j + 1) * BANKFULS
                    pe.wait_ge(turned_read[b], u * BANKFULS + (i + 1 - b) // 2)
                for batch in range(BATCHES):
                    b = batch % 2
                    wait(pe, dots_read[b], u * READS + (j * BATCHES + batch) // 2)
                    for x in range(BATCH_GROUPS):
                        at = (batch * BATCH_GROUPS + x) * P
                        four = E[:, q, j, at : at + P]
                        last = nc.tensor.matmul(
                            dots[b][: P - SLOT + VECTORS, x, : SAMPLES_PER_GROUP * VECTORS].rearrange(
                                "p (s m) -> p s m", m=VECTORS
                            ),
                            four[:, : P - SLOT + VECTORS],
                            four.rearrange("p (s m) -> p s m", m=SLOT)[:, :, :VECTORS],
                            start=True, stop=True,
                        )
                    last.then_inc(dots_done[b], 1)

            def mlp(use, bank_of, pairs_count, dense_cols, cols):
                n = cols.stop - cols.start
                pe.wait_ge(w1_dense_ready, 1)
                pe.wait_ge(weights_landed, 16 * WEIGHT_LOADS)
                for i in range(H1_CHUNKS):
                    bank = bank_of(i)[:, :n]
                    pe.wait_ge(acc_read, use + (i - 1))
                    outs = slice(i * P, (i + 1) * P)
                    nc.tensor.matmul(bank, w1_dense[:, outs], dense_cols, start=True, stop=False)
                    if i == 0:
                        pe.wait_ge(pairs_landed, pairs_count)
                    for c in range(PAIR_CHUNKS):
                        last = nc.tensor.matmul(
                            bank, w1_pair[:PAIR_ROWS, c, outs], pairs_t[:PAIR_ROWS, c, cols],
                            start=False, stop=(c == PAIR_CHUNKS - 1),
                        )
                    last.then_inc(mlp_done, 1)
                for i in range(H2_CHUNKS):
                    bank = bank_of(H1_CHUNKS + i)[:, :n]
                    for c in range(H1_CHUNKS):
                        pe.wait_ge(acc_read, use + (max(c + 1, H1_CHUNKS - 1) if i == 0 else H1_CHUNKS))
                        last = nc.tensor.matmul(
                            bank, w2_sb[:, c, i * P : (i + 1) * P], h1[:, c, cols],
                            start=(c == 0), stop=(c == H1_CHUNKS - 1),
                        )
                    last.then_inc(mlp_done, 1)

            def sum_scores(mlps, bank, tiles):
                pe.wait_ge(scores_done, mlps)
                for x, j in enumerate(tiles):
                    last = nc.tensor.matmul(bank[:, x : x + 1], scores[:, j, :], ones[:], start=True, stop=True)
                last.then_inc(mlp_done, 1)

            def unit(u, q):
                for j in range(TILES_PER_UNIT):
                    for kind, x in tile_steps(u, j):
                        if kind == "turn":
                            turn(u, j, x)
                        elif kind == "scores":
                            sum_scores(u, scores_bank(u), range(TILES_PER_UNIT))
                        else:
                            lookup(u + 1, lookup_use(u, x), lookup_bank(u, x), x)
                    dot_products(u, q, j)
                    if j == 0 and not (isinstance(u, int) and u == 0):
                        mlp(
                            mlp_use(u - 1), lambda i: mlp_bank(u - 1, i), u * 64,
                            dense_t[:, 1 - q, :, :, :].rearrange("p s j g -> p (s j g)"), slice(0, UNIT),
                        )

            all_units(pe, unit)
            for j in range(TILES_PER_UNIT):
                mlp(
                    mlp_use(UNITS - 1) + j * ACC_MLP, lambda i: last_bank(j, i), (UNITS + j) * 64,
                    dense_t[:, 1, :, j, :], slice(j * P, (j + 1) * P),
                )
                sum_scores(UNITS + j, last_bank(j, ACC_MLP - 1), range(j, j + 1))


def kernel(**inputs):
    import concourse.bacc as bacc
    from concourse.bass_utils import run_bass_kernel_spmd

    arrays = {k: np.ascontiguousarray(v) for k, v in inputs.items()}
    ids = arrays["ids"]
    spread = ids.reshape(P, UNITS, TILES_PER_UNIT, FEATURES)[:, :, :, ONE_HOT].transpose(1, 3, 2, 0)
    placed = {
        "dense_in": arrays["r_dense_features"],
        "ids_in": ids,
        "one_hot_ids_in": np.pad(spread.reshape(UNITS, ONE_HOT_TABLES * UNIT), ((0, 1), (0, 0))),
        "w1_in": np.ascontiguousarray(arrays["W_top1"][top1_row_order()]),
        "w2_in": arrays["W_top2"],
        "mlp_columns_in": np.concatenate(
            [arrays[name].reshape(-1, P).T for name in ("b_top1", "b_top2", "W_top3")], axis=1
        ),
    }
    placed.update({f"table{f}_in": arrays[f"tbl_{f}"] for f in range(FEATURES)})

    nc = bacc.Bacc("TRN2", target_bir_lowering=False, num_devices=1)
    ap = {
        name: nc.dram_tensor(name, a.shape, mybir.dt.from_np(a.dtype), kind="ExternalInput").ap()
        for name, a in placed.items()
    }
    out = nc.dram_tensor("out", (BATCH, 1), F32, kind="ExternalOutput").ap()
    dlrm_tower(
        nc, ap["dense_in"], ap["ids_in"], ap["one_hot_ids_in"], [ap[f"table{f}_in"] for f in range(FEATURES)],
        ap["w1_in"], ap["w2_in"], ap["mlp_columns_in"], out,
    )
    result = run_bass_kernel_spmd(nc, [placed], core_ids=[0])
    return result.results[0]["out"]
```

```python
from contextlib import ExitStack

import numpy as np

import concourse.bass as bass
from concourse import mybir

F32 = mybir.dt.float32
F32R = mybir.dt.float32r
I32 = mybir.dt.int32
ALU = mybir.AluOpType
ACT = mybir.ActivationFunctionType

P = 128
FEATURES = 26
VECTORS = FEATURES + 1
DIM = 128
BATCH = 2048
TILES = BATCH // P
TILES_PER_UNIT = 2
UNITS = TILES // TILES_PER_UNIT
UNIT = TILES_PER_UNIT * P

ONE_HOT = [1, 10, 13, 14, 15, 22, 0]
GATHERED = [f for f in range(FEATURES) if f not in ONE_HOT]
ONE_HOT_TABLES = len(ONE_HOT)
ORDER = [0] + [f + 1 for f in GATHERED] + [f + 1 for f in ONE_HOT]
TRANSPOSED = 1 + len(GATHERED)
PER_BANK = 4
BANKFULS = TRANSPOSED // PER_BANK

SLOT = 32
SAMPLES_PER_GROUP = P // SLOT
GROUPS = P // SAMPLES_PER_GROUP
UNIT_GROUPS = TILES_PER_UNIT * GROUPS
BATCH_GROUPS = 8
BATCHES = GROUPS // BATCH_GROUPS

ROW_STEP = VECTORS + 1
PAIR_J = VECTORS - 1
PAIR_K = (VECTORS - 1) // 2
PAIRS = VECTORS * (VECTORS - 1) // 2
PAIR_CHUNKS = 3
PAIR_ROWS = PAIRS // PAIR_CHUNKS
J_PER_CHUNK = PAIR_ROWS // PAIR_K

HIDDEN1 = 512
HIDDEN2 = 256
H1_CHUNKS = HIDDEN1 // P
H2_CHUNKS = HIDDEN2 // P

ONE_HOT_RING = 12
PREFILL = 8
BEFORE_SCORES = 10


def chunking(rows):
    chunks = -(-rows // P)
    while rows % chunks:
        chunks += 1
    return chunks, rows // chunks


def pair_rows():
    rows = []
    for c in range(PAIR_CHUNKS):
        js = range(c * J_PER_CHUNK, min((c + 1) * J_PER_CHUNK, PAIR_J))
        flat = [ROW_STEP * j + k for j in js for k in range(1, PAIR_K + 1)]
        rows += flat
    rows += [ROW_STEP * j + PAIR_K + 1 for j in range(PAIRS - PAIR_J * PAIR_K)]
    return [(x // VECTORS, x % VECTORS) for x in rows]


def top1_row_order():
    place = {}
    for n in range(VECTORS):
        for m in range(n + 1, VECTORS):
            place[n, m] = DIM + len(place)
    pairs = []
    for n, m in pair_rows():
        a, b = sorted((ORDER[n], ORDER[m]))
        pairs.append(place[a, b])
    return list(range(DIM)) + list(range(DIM + PAIRS, 2 * DIM + PAIRS)) + pairs


def dlrm_tower(nc, dense, ids, one_hot_ids, tables, w1, w2, mlp_columns, out):
    early = range(ONE_HOT_TABLES // 2 + 1)
    late = range(len(early), ONE_HOT_TABLES)
    chunks_of, rows_of = zip(*(chunking(tables[f].shape[0]) for f in ONE_HOT))
    total_chunks = sum(chunks_of)
    first_chunk = [sum(chunks_of[:k]) for k in range(ONE_HOT_TABLES)]
    early_chunks = first_chunk[late.start]
    max_chunks = max(chunks_of)
    chunk_kinds = sorted(set(chunks_of))

    dense_v = dense.rearrange("(p t) d -> p t d", t=TILES)
    ids_v = ids.rearrange("(p t) f -> p (t f)", t=TILES)
    out_v = out.rearrange("(p t) x -> p (t x)", t=TILES)
    w1_pairs = w1[2 * DIM :, :].rearrange("(c r) o -> r c o", r=PAIR_ROWS)
    products = nc.dram_tensor("products_scratch", [VECTORS * VECTORS, UNIT], F32).ap()
    products_store = products.rearrange("(n m) (s g) -> n m s g", m=VECTORS, g=UNIT_GROUPS)
    products_store_tile = products.rearrange(
        "(n m) (j s g) -> n m j s g", m=VECTORS, j=TILES_PER_UNIT, g=GROUPS
    )
    products_diag = products[0 : PAIR_J * ROW_STEP, :].rearrange("(j k) x -> j k x", k=ROW_STEP)

    ctx = ExitStack()
    with ctx:

        def sb(name, shape, dt=F32):
            return ctx.enter_context(nc.sbuf_tensor(name, shape, dt))

        def pb(name, shape, dt=F32):
            return ctx.enter_context(nc.psum_tensor(name, shape, dt))

        def sem(name):
            return ctx.enter_context(nc.semaphore(name))

        ids_all = sb("ids_all", [P, TILES * FEATURES], I32)
        idx = sb("idx", [P, 2, TILES_PER_UNIT * FEATURES], I32)
        rows = sb("rows", [P, TILES_PER_UNIT, TRANSPOSED, DIM])
        identity = sb("identity", [P, P])
        E = sb("E", [P, 2, TILES_PER_UNIT, P * SLOT])
        staging = E[:, 1, :, :].rearrange("p j x -> p (j x)").rearrange("p (c d) -> p c d", d=DIM)
        table_hi = sb("table_hi", [P, total_chunks, DIM], F32R)
        table_lo = sb("table_lo", [P, total_chunks, DIM], F32R)
        row_number_i = sb("row_number_i", [P, len(chunk_kinds), max_chunks], I32)
        row_number = sb("row_number", [P, len(chunk_kinds), max_chunks])
        ids_spread = [
            sb("ids_spread_early", [P, len(early), UNIT], I32), sb("ids_spread_late", [P, len(late), UNIT], I32)
        ]
        one_hot = sb("one_hot", [P, ONE_HOT_RING, UNIT], F32R)
        prods = sb("prods", [P, VECTORS, UNIT_GROUPS])
        dense_t = sb("dense_t", [P, 2, SAMPLES_PER_GROUP, TILES_PER_UNIT, GROUPS])
        pairs_t = sb("pairs_t", [P, PAIR_CHUNKS, UNIT])
        pairs_hi = sb("pairs_hi", [P, PAIR_CHUNKS, UNIT], F32R)
        pairs_lo = sb("pairs_lo", [P, PAIR_CHUNKS, UNIT], F32R)
        w1_dense = sb("w1_dense", [P, HIDDEN1])
        w1_pair_hi = sb("w1_pair_hi", [P, PAIR_CHUNKS, HIDDEN1], F32R)
        w1_pair_lo = sb("w1_pair_lo", [P, PAIR_CHUNKS, HIDDEN1], F32R)
        w1_pair = prods[:].rearrange("p m x -> p (m x)")[:PAIR_ROWS, : PAIR_CHUNKS * HIDDEN1].rearrange(
            "p (c o) -> p c o", c=PAIR_CHUNKS
        )
        w2_sb = sb("w2_sb", [P, H1_CHUNKS, HIDDEN2])
        columns = sb("columns", [P, H1_CHUNKS + 2 * H2_CHUNKS])
        b1_sb = columns[:, :H1_CHUNKS]
        b2_sb = columns[:, H1_CHUNKS : H1_CHUNKS + H2_CHUNKS]
        w3_sb = columns[:, H1_CHUNKS + H2_CHUNKS :]
        w1_last = E[:PAIR_ROWS, 0, 0, : PAIR_CHUNKS * HIDDEN1].rearrange("p (c o) -> p c o", c=PAIR_CHUNKS)
        h1 = sb("h1", [P, H1_CHUNKS, UNIT])
        w1_dense_parts = h1[:].rearrange("p c x -> p (c x)").rearrange("p (h o) -> p h o", h=2)
        h2 = sb("h2", [P, H2_CHUNKS, TILES_PER_UNIT, P])
        scores = sb("scores", [P, TILES_PER_UNIT, P])
        ones = sb("ones", [P, 1])
        y = sb("y", [P, TILES])

        turned = [pb(f"turned{b}", [P, PER_BANK, P]) for b in range(2)]
        dots = [pb(f"dots{b}", [P, BATCH_GROUPS, P]) for b in range(2)]
        acc = [pb(f"acc{b}", [P, 2 * UNIT]) for b in range(2)]

        ids0_landed = sem("ids0_landed")
        ids_landed = sem("ids_landed")
        idx_ready = sem("idx_ready")
        rows_landed = [[sem(f"rows_landed{j}_{g}") for g in range(BANKFULS)] for j in range(TILES_PER_UNIT)]
        dense_landed = sem("dense_landed")
        turned_done = [[sem(f"turned_done{j}_{g}") for g in range(BANKFULS)] for j in range(TILES_PER_UNIT)]
        turned_read = [sem(f"turned_read{b}") for b in range(2)]
        pads_zeroed = sem("pads_zeroed")
        identity_blank = sem("identity_blank")
        identity_ready = sem("identity_ready")
        iota_done = sem("iota_done")
        table_landed = [sem(f"table_landed{k}") for k in range(ONE_HOT_TABLES)]
        hi_done = sem("hi_done")
        lo_done = sem("lo_done")
        row_number_done = sem("row_number_done")
        spread_landed = [sem(f"spread_landed_{x}") for x in ("early", "late")]
        one_hot_ready = sem("one_hot_ready")
        one_hot_used = sem("one_hot_used")
        mlp_done = sem("mlp_done")
        ones_ready = sem("ones_ready")
        partial_scores_done = sem("partial_scores_done")
        scores_done = sem("scores_done")
        acc_read = sem("acc_read")
        dots_done = [sem(f"dots_done{b}") for b in range(2)]
        dots_read = [sem(f"dots_read{b}") for b in range(2)]
        last_quadrants_read = sem("last_quadrants_read")
        prods_stored = sem("prods_stored")
        pairs_landed = sem("pairs_landed")
        last_stored = sem("last_stored")
        last_landed = sem("last_landed")
        weights_landed = sem("weights_landed")
        w1_hi_done = sem("w1_hi_done")
        w1_ready = sem("w1_ready")
        w1_last_landed = sem("w1_last_landed")
        pairs_hi_done = sem("pairs_hi_done")
        pairs_ready = sem("pairs_ready")
        out_stored = sem("out_stored")
        WEIGHT_LOADS = 4
        MOVES = 16 * SAMPLES_PER_GROUP
        assert PAIR_CHUNKS + 1 == SAMPLES_PER_GROUP

        HIDDEN = H1_CHUNKS + H2_CHUNKS
        ACC_MLP = HIDDEN + 1
        PER_UNIT = ONE_HOT_TABLES + ACC_MLP
        assert PER_UNIT % 2 == 0

        def is_unit(u, which):
            return isinstance(u, int) and u == which

        def uses_before(u):
            return (u - 1) * PER_UNIT + (ONE_HOT_TABLES + len(early))

        def lookup_use(u, k):
            if is_unit(u, 0):
                return k
            if is_unit(u, 1) and k in early:
                return ONE_HOT_TABLES + k
            if k in late:
                return uses_before(u) + (k - late.start)
            return uses_before(u - 1) + (len(late) + k + HIDDEN * (k >= 1) + (k >= 2))

        def mlp_use(u):
            return uses_before(u + 1) + (len(late) + (0 if is_unit(u, UNITS - 2) else 1))

        def any_unit(u):
            return u if isinstance(u, int) else 3

        def lookup_bank(u, k):
            return acc[lookup_use(any_unit(u), k) % 2]

        def mlp_bank(u, i):
            return acc[(mlp_use(any_unit(u)) + i) % 2]

        def scores_bank(u):
            return mlp_bank(u, HIDDEN + 1)

        SCORES_AFTER = 2

        def last_use(j, i):
            return mlp_use(UNITS - 2) + (HIDDEN + j * ACC_MLP + i + (i >= SCORES_AFTER))

        def last_scores_use(j):
            return mlp_use(UNITS - 2) + (HIDDEN + j * ACC_MLP + (SCORES_AFTER if j < TILES_PER_UNIT else 0))

        def last_done(use):
            return use + 1 - mlp_use(UNITS - 2) + (UNITS - 2) * ACC_MLP

        SP_PARTS, POOL_PARTS = [0, 1, 2], [3]
        quadrants_of_last = [range(SAMPLES_PER_GROUP // 2), range(SAMPLES_PER_GROUP // 2, SAMPLES_PER_GROUP)]
        READS = BATCHES * TILES_PER_UNIT // 2

        def e_out(q, j, n0, n):
            v = E[:, q, j, :].rearrange("p (g s n) -> p n s g", n=SLOT, s=SAMPLES_PER_GROUP)
            return v[:, n0 : n0 + n, :, :]

        def ahead(engine, count):
            if not isinstance(count, int):
                engine.compute_val(count)
            return count

        def wait(engine, semaphore, count):
            if not (isinstance(count, int) and count == 0):
                engine.wait_ge(semaphore, count)

        def all_units(engine, unit):
            unit(0, 0)
            with engine.Fori(0, UNITS // 2 - 1) as pair:
                for q in (1, 0):
                    unit(pair * 2 + (2 - q), q)
            unit(UNITS - 1, 1)

        block = ctx.enter_context(nc.Block())

        def load_pairs(engine, part, cols, landed):
            if part < PAIR_CHUNKS:
                j0 = part * J_PER_CHUNK
                j1 = min(j0 + J_PER_CHUNK, PAIR_J)
                dst = pairs_t[0 : (j1 - j0) * PAIR_K, part, cols]
                src = products_diag[j0:j1, 1 : PAIR_K + 1, cols]
            else:
                main = (PAIR_J - (PAIR_CHUNKS - 1) * J_PER_CHUNK) * PAIR_K
                dst = pairs_t[main:PAIR_ROWS, PAIR_CHUNKS - 1, cols]
                src = products_diag[0 : PAIR_ROWS - main, PAIR_K + 1, cols]
            engine.dma_start(dst, src).then_inc(landed, 16)

        def store_tile(engine, j, s, stored):
            engine.dma_start(
                products_store_tile[:, :, j, s, :],
                prods[s * SLOT : s * SLOT + VECTORS, :, j * GROUPS : (j + 1) * GROUPS],
            ).then_inc(stored, 16)

        def move_last_tile(engine, parts, stored, landed):
            for b in range(2):
                engine.wait_ge(dots_read[b], UNITS * READS)
            engine.wait_ge(last_quadrants_read, 1)
            engine.wait_ge(pairs_landed, UNITS * MOVES)
            for s in parts:
                store_tile(engine, 1, s, stored)
            engine.wait_ge(prods_stored, UNITS * MOVES + 16 * len(SP_PARTS))
            engine.wait_ge(last_stored, 16 * len(POOL_PARTS))
            engine.wait_ge(acc_read, mlp_use(UNITS - 2) + H1_CHUNKS)
            for part in parts:
                load_pairs(engine, part, slice(P, UNIT), landed)

        @block.gpsimd
        def _(pool):
            nc.gpsimd.memset(identity[:], 0.0).then_inc(identity_blank, 1)
            for kind, chunks in enumerate(chunk_kinds):
                nc.gpsimd.iota(
                    row_number_i[:, kind, :chunks], pattern=[[1, chunks]], base=0, channel_multiplier=chunks
                ).then_inc(iota_done, 1)
            pool.wait_ge(identity_blank, 1)
            nc.gpsimd.affine_select(
                out=identity[:], in_=identity[:], compare_op=ALU.not_equal, fill=1.0, base=0,
                pattern=[[-1, P]], channel_multiplier=1,
            ).then_inc(identity_ready, 1)
            def unit(u, q):
                unit_count = ahead(pool, u)
                for j in range(TILES_PER_UNIT):
                    for i, f in enumerate(GATHERED):
                        n = i + 1
                        if n == 1 or n % PER_BANK == 0:
                            pool.wait_ge(ids0_landed, 16)
                            if n == 1 and j == 0 and not is_unit(u, 0):
                                pool.wait_ge(idx_ready, unit_count)
                            wait(pool, turned_done[j][n // PER_BANK], unit_count)
                        col = j * FEATURES + f
                        pool.indirect_dma_start(
                            out=rows[:, j, n, :], out_offset=None, in_=tables[f],
                            in_offset=bass.IndirectOffsetOnAxis(ap=idx[:, q, col : col + 1], axis=0),
                        ).then_inc(rows_landed[j][n // PER_BANK], 16)

            all_units(pool, unit)
            move_last_tile(pool, POOL_PARTS, last_stored, last_landed)

        @block.sync
        def _(sp):
            sp.dma_start(idx[:, 0, :], ids_v[:, : TILES_PER_UNIT * FEATURES]).then_inc(ids0_landed, 16)
            sp.dma_start(ids_all[:], ids_v).then_inc(ids_landed, 16)

            def load_spread(u, part):
                if not is_unit(u, 0):
                    made_count = ahead(sp, u * total_chunks if part else (u - 1) * total_chunks + early_chunks)
                    sp.wait_ge(table_landed[0], 16)
                    sp.wait_ge(one_hot_ready, made_count)
                first, tables_here = (late.start, len(late)) if part else (0, len(early))
                sp.dma_start(
                    ids_spread[part][:].rearrange("p k x -> p (k x)"),
                    one_hot_ids[bass.ds(u, 1), first * UNIT : (first + tables_here) * UNIT].partition_broadcast(P),
                ).then_inc(spread_landed[part], 16)

            def load_dense(u):
                if not is_unit(u, 0):
                    turned_count = ahead(sp, u)
                    sp.wait_ge(table_landed[0], 16)
                    for j in range(TILES_PER_UNIT):
                        sp.wait_ge(turned_done[j][0], turned_count)
                sp.dma_start(
                    rows[:, :, 0, :], dense_v[:, bass.ds(u * TILES_PER_UNIT, TILES_PER_UNIT), :]
                ).then_inc(dense_landed, 16)

            def load_table(k):
                sp.dma_start(
                    staging[: rows_of[k], first_chunk[k] : first_chunk[k] + chunks_of[k], :],
                    tables[ONE_HOT[k]].rearrange("(r c) d -> r c d", c=chunks_of[k]),
                ).then_inc(table_landed[k], 16)

            load_table(0)
            load_spread(0, 0)
            load_table(1)
            load_spread(0, 1)
            load_dense(0)
            for k in range(2, ONE_HOT_TABLES):
                sp.wait_ge(table_landed[k - 2], 16)
                load_table(k)
            sp.wait_ge(table_landed[ONE_HOT_TABLES - 1], 16)
            load_spread(1, 0)
            sp.dma_start(
                w1_dense_parts[:], w1[0 : 2 * DIM, :].rearrange("(h p) o -> p h o", p=DIM)
            ).then_inc(weights_landed, 16)
            sp.dma_start(w1_pair, w1_pairs).then_inc(weights_landed, 16)
            sp.dma_start(w2_sb[:], w2.rearrange("(c p) o -> p c o", p=P)).then_inc(weights_landed, 16)
            sp.dma_start(columns[:], mlp_columns).then_inc(weights_landed, 16)

            def unit(u, q):
                if is_unit(u, UNITS - 1):
                    last_unit()
                else:
                    whole_unit(u)

            def whole_unit(u):
                load_spread(u + 1, 1)
                load_dense(u + 1)
                load_spread(u + 2, 0)
                dots_count = ahead(sp, (u + 1) * READS)
                pairs_count = ahead(sp, u * MOVES)
                for b in range(2):
                    sp.wait_ge(dots_read[b], dots_count)
                wait(sp, pairs_landed, pairs_count)
                for s in range(SAMPLES_PER_GROUP):
                    sp.dma_start(
                        products_store[:, :, s, :], prods[s * SLOT : s * SLOT + VECTORS, :, :]
                    ).then_inc(prods_stored, 16)
                free_count = ahead(sp, 0 if is_unit(u, 0) else mlp_use(u - 1) + H1_CHUNKS)
                sp.wait_ge(prods_stored, (u + 1) * MOVES)
                wait(sp, acc_read, free_count)
                for part in range(PAIR_CHUNKS + 1):
                    load_pairs(sp, part, slice(0, UNIT), pairs_landed)

            def last_unit():
                u = UNITS - 1
                for b in range(2):
                    sp.wait_ge(dots_done[b], u * READS)
                sp.dma_start(w1_last, w1_pairs).then_inc(w1_last_landed, 16)
                for b in range(2):
                    sp.wait_ge(dots_read[b], u * READS + READS // 2)
                sp.wait_ge(pairs_landed, u * MOVES)
                for s in range(SAMPLES_PER_GROUP):
                    store_tile(sp, 0, s, prods_stored)
                sp.wait_ge(prods_stored, (u + 1) * MOVES)
                sp.wait_ge(acc_read, mlp_use(u - 1) + H1_CHUNKS)
                for part in range(PAIR_CHUNKS + 1):
                    load_pairs(sp, part, slice(0, P), pairs_landed)
                move_last_tile(sp, SP_PARTS, prods_stored, pairs_landed)

            all_units(sp, unit)
            sp.wait_ge(acc_read, last_scores_use(TILES_PER_UNIT) + 1)
            sp.dma_start(out_v, y[:]).then_inc(out_stored, 16)
            sp.wait_ge(out_stored, 16)

        def tile_steps(u, j):
            if j == 0:
                if is_unit(u, 0):
                    return
                lookups = [(u, k) for k in late]
                if not is_unit(u, UNITS - 1):
                    lookups.append((u + 1, 0))
                after_bankful = {0: 1, 2: 1, 3: 1, 4: len(lookups) - 3}
            else:
                if is_unit(u, UNITS - 1):
                    return
                lookups = [(u + 1, k) for k in early[0 if is_unit(u, 0) else 1 :]]
                after_bankful = {1: 1, 3: 1, 4: len(lookups) - 2}
            for g in range(BANKFULS):
                yield "turn", g
                for _ in range(after_bankful.get(g, 0)):
                    yield "look up", lookups.pop(0)
                if g == 1 and j == 1 and not is_unit(u, 0):
                    yield "scores", None

        def hidden_steps(u, j):
            split = BANKFULS if is_unit(u, UNITS - 1) else HIDDEN
            return range(split) if j == 0 else range(split, HIDDEN)

        def turns_after(i):
            return [i] if i < BANKFULS else []

        def batch_quadrants(j, batch, b, quadrants=range(SAMPLES_PER_GROUP)):
            g0 = j * GROUPS + batch * BATCH_GROUPS
            for s in quadrants:
                lo = s * SLOT
                src = dots[b][lo : lo + VECTORS, :, s * VECTORS : (s + 1) * VECTORS]
                dst = prods[lo : lo + VECTORS, :, g0 : g0 + BATCH_GROUPS].rearrange("p m g -> p g m")
                yield dst, src

        @block.scalar
        def _(act):
            def lookup_out(u, bank, q, k):
                act.wait_ge(one_hot_used, u * total_chunks + first_chunk[k] + chunks_of[k])
                n = TRANSPOSED + k
                for j in range(TILES_PER_UNIT):
                    dst = E[:, q, j, :].rearrange("p (g s n) -> p n s g", n=SLOT, s=SAMPLES_PER_GROUP)
                    last = nc.scalar.copy(
                        dst[:, n, :, :], bank[:, j * P : (j + 1) * P].rearrange("p (s g) -> p s g", g=GROUPS)
                    )
                last.then_inc(acc_read, 1)

            def turn_out(u, q, j, g):
                act.wait_ge(turned_done[j][g], u + 1)
                bank = (j * BANKFULS + g) % 2
                src = turned[bank][:, :, :].rearrange("p n (s g) -> p n s g", g=GROUPS)
                if g == 0:
                    nc.scalar.copy(dense_t[:, q, :, j, :], src[:, 0, :, :])
                nc.scalar.copy(e_out(q, j, g * PER_BANK, PER_BANK), src).then_inc(turned_read[bank], 1)

            def prologue_out(k):
                lookup_out(0, acc[k % 2], 0, k)
                if 1 <= k <= BANKFULS:
                    turn_out(0, 0, 0, k - 1)

            for k in range(ONE_HOT_TABLES):
                act.wait_ge(table_landed[k], 16)
                r, c, c0 = rows_of[k], chunks_of[k], first_chunk[k]
                nc.scalar.copy(
                    table_hi[:r, c0 : c0 + c, :], staging[:r, c0 : c0 + c, :]
                ).then_inc(hi_done, 1)
                if k >= 1:
                    prologue_out(k - 1)
            act.wait_ge(weights_landed, 16 * WEIGHT_LOADS)
            nc.scalar.copy(w1_pair_hi[:PAIR_ROWS], w1_pair).then_inc(w1_hi_done, 1)
            prologue_out(ONE_HOT_TABLES - 1)

            def hidden_out(done, bank, cols, hidden, after):
                act.wait_ge(weights_landed, 16 * WEIGHT_LOADS)
                n = cols.stop - cols.start
                for i in hidden:
                    act.wait_ge(mlp_done, done(i))
                    src = bank(i)[:, :n]
                    if i < H1_CHUNKS:
                        last = nc.scalar.activation(h1[:, i, cols], src, ACT.Relu, bias=b1_sb[:, i : i + 1])
                    else:
                        c = i - H1_CHUNKS
                        if n == UNIT:
                            dst = h2[:, c, :, :].rearrange("p j (s g) -> p s j g", g=GROUPS)
                            src = src.rearrange("p (s j g) -> p s j g", j=TILES_PER_UNIT, g=GROUPS)
                        else:
                            dst = h2[:, c, cols.start // P, :]
                        last = nc.scalar.activation(dst, src, ACT.Relu, bias=b2_sb[:, c : c + 1])
                    last.then_inc(acc_read, 1)
                    after(i)

            def score_out(done, bank, col, n):
                act.wait_ge(mlp_done, done)
                nc.scalar.copy(y[:, bass.ds(col, n)], bank[:, :n]).then_inc(acc_read, 1)

            def unit(u, q):
                for j in range(TILES_PER_UNIT):
                    for kind, x in tile_steps(u, j):
                        if kind == "turn":
                            turn_out(u, q, j, x)
                        elif kind == "scores":
                            score_out(
                                u * ACC_MLP, scores_bank(u - 1), (u - 1) * TILES_PER_UNIT, TILES_PER_UNIT
                            )
                        else:
                            to, k = x
                            lookup_out(to, lookup_bank(to, k), q if to is u else 1 - q, k)
                    if j == 0 and is_unit(u, 0):
                        act.wait_ge(w1_ready, 1)
                    elif j == 0:
                        act.wait_ge(prods_stored, u * MOVES)
                    for batch in range(0, BATCHES, 2):
                        act.wait_ge(dots_done[0], u * READS + ((j * BATCHES + batch) // 2 + 1))
                        for dst, src in batch_quadrants(j, batch, 0):
                            last = nc.scalar.copy(dst, src)
                        last.then_inc(dots_read[0], 1)
                        if j == 0 and batch == 0 and not is_unit(u, 0):
                            act.wait_ge(pairs_landed, u * MOVES)
                            nc.scalar.copy(pairs_hi[:PAIR_ROWS], pairs_t[:PAIR_ROWS]).then_inc(pairs_hi_done, 1)
                    if is_unit(u, UNITS - 1) and j == 1:
                        act.wait_ge(dots_done[1], UNITS * READS)
                        for dst, src in batch_quadrants(1, BATCHES - 1, 1, quadrants_of_last[1]):
                            last = nc.scalar.copy(dst, src)
                        last.then_inc(last_quadrants_read, 1)
                    if not is_unit(u, 0):
                        unit_hidden_out(u, q, hidden_steps(u, j))

            def unit_hidden_out(u, q, hidden):

                def after(i):
                    if is_unit(u, UNITS - 1):
                        for g in turns_after(i):
                            turn_out(u, q, 1, g)

                hidden_out(
                    lambda i: (u - 1) * ACC_MLP + (i + 1), lambda i: mlp_bank(u - 1, i), slice(0, UNIT),
                    hidden, after,
                )

            def last_mlp_out(j):
                def after(i):
                    if i == SCORES_AFTER - 1:
                        last_score_out(j)

                hidden_out(
                    lambda i: last_done(last_use(j, i)), lambda i: acc[last_use(j, i) % 2],
                    slice(j * P, (j + 1) * P), range(HIDDEN), after,
                )

            def last_score_out(j):
                use = last_scores_use(j)
                col, n = ((UNITS - 2) * TILES_PER_UNIT, TILES_PER_UNIT) if j == 0 else (
                    (UNITS - 1) * TILES_PER_UNIT + (j - 1), 1
                )
                score_out(last_done(use), acc[use % 2], col, n)

            all_units(act, unit)
            for j in range(TILES_PER_UNIT):
                last_mlp_out(j)
            last_score_out(TILES_PER_UNIT)

        one_hot_order = [(k, c) for k in range(ONE_HOT_TABLES) for c in range(chunks_of[k])]

        def ring_used(u, i):
            last = i - ONE_HOT_RING
            if last < 0:
                last = max(x for x in range(total_chunks) if x % ONE_HOT_RING == i) - total_chunks
            return u * total_chunks + last + 1

        @block.vector
        def _(dve):
            def one_hots(u, first, end):
                for i in range(first, end):
                    k, c = one_hot_order[i]
                    r = rows_of[k]
                    if not (is_unit(u, 0) and i < ONE_HOT_RING):
                        dve.wait_ge(one_hot_used, ring_used(u, i))
                    kind = chunk_kinds.index(chunks_of[k])
                    ids_here = ids_spread[1][:r, k - late.start, :] if k in late else ids_spread[0][:r, k, :]
                    nc.vector.tensor_scalar(
                        one_hot[:r, i % ONE_HOT_RING, :], ids_here, row_number[:r, kind, c : c + 1],
                        None, ALU.is_equal,
                    ).then_inc(one_hot_ready, 1)

            def zero_pads(q):
                nc.vector.memset(
                    E[:, q, :, :].rearrange("p j (x n) -> p (j x) n", n=SLOT)[:, :, VECTORS:SLOT], 0.0
                ).then_inc(pads_zeroed, 1)

            def make_scores(mlps, read, tile):
                dve.wait_ge(acc_read, read)
                nc.vector.tensor_scalar(
                    scores[:, tile, :], h2[:, 0, tile, :], w3_sb[:, 0:1], None, ALU.mult
                ).then_inc(partial_scores_done, 1)
                dve.wait_ge(partial_scores_done, mlps + 1)
                nc.vector.scalar_tensor_tensor(
                    scores[:, tile, :], h2[:, 1, tile, :], w3_sb[:, 1:2], scores[:, tile, :], ALU.mult, ALU.add
                ).then_inc(scores_done, 1)

            def place_ids(u, q):
                per_unit = TILES_PER_UNIT * FEATURES
                nc.vector.tensor_copy(idx[:, q, :], ids_all[:, bass.ds(u * per_unit, per_unit)]).then_inc(idx_ready, 1)

            nc.vector.memset(ones[:], 1.0).then_inc(ones_ready, 1)
            zero_pads(0)
            dve.wait_ge(iota_done, len(chunk_kinds))
            for kind, chunks in enumerate(chunk_kinds):
                nc.vector.tensor_copy(
                    row_number[:, kind, :chunks], row_number_i[:, kind, :chunks]
                ).then_inc(row_number_done, 1)
            dve.wait_ge(row_number_done, len(chunk_kinds))
            for k in range(ONE_HOT_TABLES):
                r, c, c0 = rows_of[k], chunks_of[k], first_chunk[k]
                dve.wait_ge(table_landed[k], 16)
                dve.wait_ge(hi_done, k + 1)
                nc.vector.tensor_tensor(
                    table_lo[:r, c0 : c0 + c, :], staging[:r, c0 : c0 + c, :],
                    table_hi[:r, c0 : c0 + c, :].bitcast(F32), ALU.subtract,
                ).then_inc(lo_done, 1)
                if k in (early.start, late.start):
                    dve.wait_ge(spread_landed[1 if k in late else 0], 16)
                one_hots(0, c0, c0 + c)
            dve.wait_ge(weights_landed, 16 * WEIGHT_LOADS)
            dve.wait_ge(w1_hi_done, 1)
            nc.vector.tensor_tensor(
                w1_pair_lo[:PAIR_ROWS], w1_pair, w1_pair_hi[:PAIR_ROWS].bitcast(F32), ALU.subtract
            ).then_inc(w1_ready, 1)
            dve.wait_ge(spread_landed[0], 2 * 16)
            one_hots(1, 0, PREFILL)

            def unit(u, q):
                for j in range(TILES_PER_UNIT):
                    if j == 0 and is_unit(u, 0):
                        made = ONE_HOT_RING
                        one_hots(1, PREFILL, made)
                    elif j == 0:
                        one_hots(u, early_chunks + PREFILL, total_chunks)
                        if not is_unit(u, UNITS - 1):
                            dve.wait_ge(spread_landed[0], (u + 2) * 16)
                            made = first_chunk[1]
                            one_hots(u + 1, 0, made)
                    else:
                        if not (is_unit(u, 0) or is_unit(u, UNITS - 1)):
                            one_hots(u + 1, made, made + BEFORE_SCORES)
                            made += BEFORE_SCORES
                            make_scores(u - 1, mlp_use(u - 1) + HIDDEN, slice(0, TILES_PER_UNIT))
                        if not is_unit(u, UNITS - 1):
                            one_hots(u + 1, made, early_chunks)
                    if j == 0 and is_unit(u, 0):
                        dve.wait_ge(w1_ready, 1)
                    elif j == 0:
                        dve.wait_ge(prods_stored, u * MOVES)
                    for batch in range(1, BATCHES, 2):
                        dve.wait_ge(dots_done[1], u * READS + ((j * BATCHES + batch) // 2 + 1))
                        last_batch = is_unit(u, UNITS - 1) and j == 1 and batch == BATCHES - 1
                        mine = quadrants_of_last[0] if last_batch else range(SAMPLES_PER_GROUP)
                        for dst, src in batch_quadrants(j, batch, 1, mine):
                            last = nc.vector.tensor_copy(dst, src)
                        last.then_inc(dots_read[1], 1)
                        if j == 0 and batch == 1 and not is_unit(u, UNITS - 1):
                            dve.wait_ge(ids_landed, 16)
                            place_ids(u + 1, 1 - q)
                        if j == 0 and batch == 1 and not is_unit(u, 0):
                            dve.wait_ge(pairs_hi_done, u)
                            nc.vector.tensor_tensor(
                                pairs_lo[:PAIR_ROWS], pairs_t[:PAIR_ROWS], pairs_hi[:PAIR_ROWS].bitcast(F32),
                                ALU.subtract,
                            ).then_inc(pairs_ready, 1)
                        if j == 1 and batch == 1 and not is_unit(u, UNITS - 1):
                            dve.wait_ge(spread_landed[1], (u + 2) * 16)
                            one_hots(u + 1, early_chunks, early_chunks + PREFILL)
                    if j == 0 and is_unit(u, 0):
                        dve.wait_ge(lo_done, ONE_HOT_TABLES)
                        zero_pads(1)
                        nc.vector.tensor_tensor(
                            w1_dense[:], w1_dense_parts[:, 0, :], w1_dense_parts[:, 1, :], ALU.add
                        ).then_inc(w1_ready, 1)

            all_units(dve, unit)
            u = UNITS - 2
            make_scores(u, mlp_use(u) + HIDDEN, slice(0, TILES_PER_UNIT))
            for j in range(TILES_PER_UNIT):
                make_scores(UNITS - 1 + j, last_use(j, HIDDEN - 1) + 1, slice(j, j + 1))

        @block.tensor
        def _(pe):
            def lookup(u, use, bank, k):
                c0 = first_chunk[k]
                if not (isinstance(use, int) and use < 2):
                    pe.wait_ge(acc_read, use - 1)
                for i in range(c0, c0 + chunks_of[k]):
                    r = rows_of[k]
                    pe.wait_ge(one_hot_ready, u * total_chunks + i + 1)
                    hot = one_hot[:r, i % ONE_HOT_RING, :]
                    nc.tensor.matmul(bank[:, :UNIT], table_hi[:r, i, :], hot, start=(i == c0), stop=False)
                    nc.tensor.matmul(
                        bank[:, :UNIT], table_lo[:r, i, :], hot, start=False, stop=(i == c0 + chunks_of[k] - 1)
                    ).then_inc(one_hot_used, 1)

            def turn(u, j, g):
                i = j * BANKFULS + g
                if g == 0:
                    pe.wait_ge(dense_landed, (u + 1) * 16)
                    pe.wait_ge(rows_landed[j][g], (u + 1) * (16 * (PER_BANK - 1)))
                else:
                    pe.wait_ge(rows_landed[j][g], (u + 1) * (16 * PER_BANK))
                wait(pe, turned_read[i % 2], u * BANKFULS + i // 2)
                for n in range(PER_BANK):
                    last = nc.tensor.transpose(
                        turned[i % 2][:, n, :], rows[:, j, g * PER_BANK + n, :], identity[:]
                    )
                last.then_inc(turned_done[j][g], 1)

            pe.wait_ge(identity_ready, 1)
            for k in range(ONE_HOT_TABLES):
                pe.wait_ge(lo_done, k + 1)
                lookup(0, k, acc[k % 2], k)
                if 1 <= k <= BANKFULS:
                    turn(0, 0, k - 1)
            pe.wait_ge(ones_ready, 1)

            def dot_products(u, q, j):
                if j == 0:
                    pe.wait_ge(acc_read, lookup_use(u, ONE_HOT_TABLES - 1) + 1)
                    pe.wait_ge(pads_zeroed, 1 if is_unit(u, 0) else 2)
                for b in range(2):
                    i = (j + 1) * BANKFULS
                    pe.wait_ge(turned_read[b], u * BANKFULS + (i + 1 - b) // 2)
                for batch in range(BATCHES):
                    b = batch % 2
                    wait(pe, dots_read[b], u * READS + (j * BATCHES + batch) // 2)
                    for x in range(BATCH_GROUPS):
                        at = (batch * BATCH_GROUPS + x) * P
                        four = E[:, q, j, at : at + P]
                        last = nc.tensor.matmul(
                            dots[b][: P - SLOT + VECTORS, x, : SAMPLES_PER_GROUP * VECTORS].rearrange(
                                "p (s m) -> p s m", m=VECTORS
                            ),
                            four[:, : P - SLOT + VECTORS],
                            four.rearrange("p (s m) -> p s m", m=SLOT)[:, :, :VECTORS],
                            start=True, stop=True,
                        )
                    last.then_inc(dots_done[b], 1)

            def unit_use(u):
                return lambda i: mlp_use(u) + i

            def first_layer(use, bank_of, dense_cols, add_pairs, n, after):
                pe.wait_ge(w1_ready, 2)
                pe.wait_ge(weights_landed, 16 * WEIGHT_LOADS)
                for i in range(H1_CHUNKS):
                    bank = bank_of(i)[:, :n]
                    pe.wait_ge(acc_read, use(i) - 1)
                    outs = slice(i * P, (i + 1) * P)
                    nc.tensor.matmul(bank, w1_dense[:, outs], dense_cols, start=True, stop=False)
                    add_pairs(i, bank, outs).then_inc(mlp_done, 1)
                    after(i)

            def split_pairs(mlps):

                def add(i, bank, outs):
                    if i == 0:
                        pe.wait_ge(pairs_ready, mlps + 1)
                    for c in range(PAIR_CHUNKS):
                        for w, x in ((w1_pair_hi, pairs_hi), (w1_pair_lo, pairs_hi), (w1_pair_hi, pairs_lo)):
                            last = nc.tensor.matmul(
                                bank, w[:PAIR_ROWS, c, outs], x[:PAIR_ROWS, c, :],
                                start=False, stop=(c == PAIR_CHUNKS - 1 and x is pairs_lo),
                            )
                    return last

                return add

            def whole_pairs(j):

                def add(i, bank, outs):
                    if i == 0:
                        pe.wait_ge(w1_last_landed, 16)
                        pe.wait_ge(pairs_landed, UNITS * MOVES + j * 16 * len(SP_PARTS))
                        if j == 1:
                            pe.wait_ge(last_landed, 16 * len(POOL_PARTS))
                    for c in range(PAIR_CHUNKS):
                        last = nc.tensor.matmul(
                            bank, w1_last[:, c, outs], pairs_t[:PAIR_ROWS, c, j * P : (j + 1) * P],
                            start=False, stop=(c == PAIR_CHUNKS - 1),
                        )
                    return last

                return add

            def second_layer(use, bank_of, cols, results, after):
                n = cols.stop - cols.start
                for i in results:
                    bank = bank_of(i)[:, :n]
                    pe.wait_ge(acc_read, use(i) - 1)
                    outs = slice((i - H1_CHUNKS) * P, (i - H1_CHUNKS + 1) * P)
                    for c in range(H1_CHUNKS):
                        if i == H1_CHUNKS and c == H1_CHUNKS - 1:
                            pe.wait_ge(acc_read, use(c) + 1)
                        last = nc.tensor.matmul(
                            bank, w2_sb[:, c, outs], h1[:, c, cols], start=(c == 0), stop=(c == H1_CHUNKS - 1)
                        )
                    last.then_inc(mlp_done, 1)
                    after(i)

            def sum_scores(mlps, bank, tiles):
                pe.wait_ge(scores_done, mlps)
                for x, j in enumerate(tiles):
                    last = nc.tensor.matmul(bank[:, x : x + 1], scores[:, j, :], ones[:], start=True, stop=True)
                last.then_inc(mlp_done, 1)

            def unit(u, q):
                for j in range(TILES_PER_UNIT):
                    for kind, x in tile_steps(u, j):
                        if kind == "turn":
                            turn(u, j, x)
                        elif kind == "scores":
                            sum_scores(u, scores_bank(u - 1), range(TILES_PER_UNIT))
                        else:
                            to, k = x
                            lookup(to, lookup_use(to, k), lookup_bank(to, k), k)
                    dot_products(u, q, j)
                    if not is_unit(u, 0) and j == 0:
                        first_layer(
                            unit_use(u - 1), lambda i: mlp_bank(u - 1, i),
                            dense_t[:, 1 - q, :, :, :].rearrange("p s j g -> p (s j g)"),
                            split_pairs(u - 1), UNIT, lambda i: turns_between(u, i),
                        )
                    if not is_unit(u, 0):
                        second_layer(
                            unit_use(u - 1), lambda i: mlp_bank(u - 1, i), slice(0, UNIT),
                            [i for i in hidden_steps(u, j) if i >= H1_CHUNKS], lambda i: turns_between(u, i),
                        )

            def turns_between(u, i):
                if is_unit(u, UNITS - 1):
                    for g in turns_after(i):
                        turn(u, 1, g)

            def last_scores(j):
                use = last_scores_use(j)
                pe.wait_ge(acc_read, use - 1)
                sum_scores(UNITS - 1 + j, acc[use % 2], range(TILES_PER_UNIT) if j == 0 else range(j - 1, j))

            all_units(pe, unit)
            for j in range(TILES_PER_UNIT):
                first_layer(
                    lambda i: last_use(j, i), lambda i: acc[last_use(j, i) % 2], dense_t[:, 1, :, j, :],
                    whole_pairs(j), P,
                    lambda i: last_scores(j) if i == SCORES_AFTER - 1 else None,
                )
                second_layer(
                    lambda i: last_use(j, i), lambda i: acc[last_use(j, i) % 2], slice(j * P, (j + 1) * P),
                    range(H1_CHUNKS, HIDDEN), lambda i: None,
                )
            last_scores(TILES_PER_UNIT)


def kernel(**inputs):
    import concourse.bacc as bacc
    from concourse.bass_utils import run_bass_kernel_spmd

    arrays = {k: np.ascontiguousarray(v) for k, v in inputs.items()}
    ids = arrays["ids"]
    spread = ids.reshape(P, UNITS, TILES_PER_UNIT, FEATURES)[:, :, :, ONE_HOT].transpose(1, 3, 2, 0)
    placed = {
        "dense_in": arrays["r_dense_features"],
        "ids_in": ids,
        "one_hot_ids_in": np.pad(spread.reshape(UNITS, ONE_HOT_TABLES * UNIT), ((0, 1), (0, 0))),
        "w1_in": np.ascontiguousarray(arrays["W_top1"][top1_row_order()]),
        "w2_in": arrays["W_top2"],
        "mlp_columns_in": np.concatenate(
            [arrays[name].reshape(-1, P).T for name in ("b_top1", "b_top2", "W_top3")], axis=1
        ),
    }
    placed.update({f"table{f}_in": arrays[f"tbl_{f}"] for f in range(FEATURES)})

    nc = bacc.Bacc("TRN2", target_bir_lowering=False, num_devices=1)
    ap = {
        name: nc.dram_tensor(name, a.shape, mybir.dt.from_np(a.dtype), kind="ExternalInput").ap()
        for name, a in placed.items()
    }
    out = nc.dram_tensor("out", (BATCH, 1), F32, kind="ExternalOutput").ap()
    dlrm_tower(
        nc, ap["dense_in"], ap["ids_in"], ap["one_hot_ids_in"], [ap[f"table{f}_in"] for f in range(FEATURES)],
        ap["w1_in"], ap["w2_in"], ap["mlp_columns_in"], out,
    )
    result = run_bass_kernel_spmd(nc, [placed], core_ids=[0])
    return result.results[0]["out"]
```
